# Optimizing a Trainium2 kernel written in Bass

```python
import numpy as np
import jax
import jax.numpy as jnp

def _softmax(x, axis=-1):
    return jax.nn.softmax(x, axis=axis)

def _gelu(x):
    return jax.nn.gelu(x, approximate=True)

def _silu(x):
    return jax.nn.silu(x)

def _sigmoid(x):
    return jax.nn.sigmoid(x)

def _layernorm(x, axis=-1, eps=1e-05):
    m = jnp.mean(x, axis=axis, keepdims=True)
    v = jnp.var(x, axis=axis, keepdims=True)
    return (x - m) / jnp.sqrt(v + eps)

def _scatter_add(tgt, idx, src, axis=0):
    return tgt.at[idx].add(src)

def _segment_sum(src, seg, n):
    return jax.ops.segment_sum(src, seg, n)
kernel_name = 'mk_rec_standalone_d1_rec_r8_b88c2e'

def setup_inputs(seed: int=0):
    np.random.seed(seed)
    _w = jnp.asarray

    def _rec_inputs():
        import jax
        import jax.numpy as jnp
        _rk = jax.random.key(seed)
        r_user = jax.random.randint(jax.random.fold_in(_rk, 1), (2048, 1), 16, 49993, jnp.int32)
        r_item = jnp.stack([jax.random.randint(jax.random.fold_in(jax.random.fold_in(_rk, 2), 0), (2048,), 1, 1000, jnp.int32), jax.random.randint(jax.random.fold_in(jax.random.fold_in(_rk, 2), 1), (2048,), 1, 1000, jnp.int32), jax.random.randint(jax.random.fold_in(jax.random.fold_in(_rk, 2), 2), (2048,), 0, 1000, jnp.int32)], axis=1)
        r_rec_his = jax.random.randint(jax.random.fold_in(_rk, 3), (2048, 200, 3), 0, 1000, jnp.int32)
        return (r_user, r_item, r_rec_his)
    r_user, r_item, r_rec_his = _rec_inputs()

    def _L0_rec_setup():
        import jax, jax.numpy as jnp
        import numpy as np
        B, L = (256, 200)
        D_FEAT = 32
        E = 3 * D_FEAT
        U = 64
        HID_ATT = 36
        H1, H2 = (200, 80)
        V_USER, V_ITEM = (6250, 1000)
        EPS = 1e-08

        def _dice(x, alpha, gamma, beta):
            mean = jnp.mean(x, axis=0, keepdims=True)
            var = jnp.var(x, axis=0, ddof=1, keepdims=True)
            xn = (x - mean) / jnp.sqrt(var + EPS) * gamma + beta
            p = jax.nn.sigmoid(xn)
            return alpha * (1.0 - p) * xn + p * xn
        key = jax.random.key(seed)
        ks = jax.random.split(key, 24)
        f = jax.random.normal
        inp = {'user': jax.random.randint(ks[0], (B, 1), 0, V_USER), 'item': jax.random.randint(ks[1], (B, 3), 0, V_ITEM), 'rec_his': jax.random.randint(ks[2], (B, L, 3), 0, V_ITEM), 'table_user': f(ks[3], (V_USER, U), dtype=jnp.float32) * 0.05, 'table_i1': f(ks[4], (V_ITEM, D_FEAT), dtype=jnp.float32) * 0.05, 'table_i2': f(ks[5], (V_ITEM, D_FEAT), dtype=jnp.float32) * 0.05, 'table_i3': f(ks[6], (V_ITEM, D_FEAT), dtype=jnp.float32) * 0.05, 'w_att1': f(ks[7], (HID_ATT, 4 * E), dtype=jnp.float32) * 0.05, 'b_att1': jnp.zeros((HID_ATT,), jnp.float32), 'w_att2': f(ks[8], (1, HID_ATT), dtype=jnp.float32) * 0.05, 'b_att2': jnp.zeros((1,), jnp.float32), 'w1': f(ks[9], (H1, 2 * E + U), dtype=jnp.float32) * 0.05, 'b1': jnp.zeros((H1,), jnp.float32), 'a1': f(ks[10], (H1,), dtype=jnp.float32) * 0.05, 'g1': jnp.ones((H1,), jnp.float32), 'be1': jnp.zeros((H1,), jnp.float32), 'w2': f(ks[11], (H2, H1), dtype=jnp.float32) * 0.05, 'b2': jnp.zeros((H2,), jnp.float32), 'a2': f(ks[12], (H2,), dtype=jnp.float32) * 0.05, 'g2': jnp.ones((H2,), jnp.float32), 'be2': jnp.zeros((H2,), jnp.float32), 'w3': f(ks[13], (1, H2), dtype=jnp.float32) * 0.05, 'b3': jnp.zeros((1,), jnp.float32)}
        return inp
    _L0_rec_all = _L0_rec_setup()
    _L0_rec_in = {k: v for k, v in _L0_rec_all.items() if k in ('table_user', 'table_i1', 'table_i2', 'table_i3', 'w_att1', 'b_att1', 'w_att2', 'b_att2', 'w1', 'b1', 'a1', 'g1', 'be1', 'w2', 'b2', 'a2', 'g2', 'be2', 'w3', 'b3')}
    del _L0_rec_all
    return {'r_user': r_user, 'r_item': r_item, 'r_rec_his': r_rec_his, 'L0_rec_table_user': _L0_rec_in['table_user'], 'L0_rec_table_i1': _L0_rec_in['table_i1'], 'L0_rec_table_i2': _L0_rec_in['table_i2'], 'L0_rec_table_i3': _L0_rec_in['table_i3'], 'L0_rec_w_att1': _L0_rec_in['w_att1'], 'L0_rec_b_att1': _L0_rec_in['b_att1'], 'L0_rec_w_att2': _L0_rec_in['w_att2'], 'L0_rec_b_att2': _L0_rec_in['b_att2'], 'L0_rec_w1': _L0_rec_in['w1'], 'L0_rec_b1': _L0_rec_in['b1'], 'L0_rec_a1': _L0_rec_in['a1'], 'L0_rec_g1': _L0_rec_in['g1'], 'L0_rec_be1': _L0_rec_in['be1'], 'L0_rec_w2': _L0_rec_in['w2'], 'L0_rec_b2': _L0_rec_in['b2'], 'L0_rec_a2': _L0_rec_in['a2'], 'L0_rec_g2': _L0_rec_in['g2'], 'L0_rec_be2': _L0_rec_in['be2'], 'L0_rec_w3': _L0_rec_in['w3'], 'L0_rec_b3': _L0_rec_in['b3']}

def reference(r_user, r_item, r_rec_his, L0_rec_table_user, L0_rec_table_i1, L0_rec_table_i2, L0_rec_table_i3, L0_rec_w_att1, L0_rec_b_att1, L0_rec_w_att2, L0_rec_b_att2, L0_rec_w1, L0_rec_b1, L0_rec_a1, L0_rec_g1, L0_rec_be1, L0_rec_w2, L0_rec_b2, L0_rec_a2, L0_rec_g2, L0_rec_be2, L0_rec_w3, L0_rec_b3):
    import jax
    import jax.numpy as jnp

    def _L0_rec_ref(user, item, rec_his, table_user, table_i1, table_i2, table_i3, w_att1, b_att1, w_att2, b_att2, w1, b1, a1, g1, be1, w2, b2, a2, g2, be2, w3, b3):
        import jax, jax.numpy as jnp
        import numpy as np
        B, L = (256, 200)
        D_FEAT = 32
        E = 3 * D_FEAT
        U = 64
        HID_ATT = 36
        H1, H2 = (200, 80)
        V_USER, V_ITEM = (6250, 1000)
        EPS = 1e-08

        def _dice(x, alpha, gamma, beta):
            mean = jnp.mean(x, axis=0, keepdims=True)
            var = jnp.var(x, axis=0, ddof=1, keepdims=True)
            xn = (x - mean) / jnp.sqrt(var + EPS) * gamma + beta
            p = jax.nn.sigmoid(xn)
            return alpha * (1.0 - p) * xn + p * xn
        user_emb = table_user[user[:, 0]]
        item_emb = jnp.concatenate([table_i1[item[:, 0]], table_i2[item[:, 1]], table_i3[item[:, 2]]], axis=1)
        ub = jnp.concatenate([table_i1[rec_his[:, :, 0]], table_i2[rec_his[:, :, 1]], table_i3[rec_his[:, :, 2]]], axis=2)
        mask = rec_his[:, :, 0] == 0
        q = jnp.broadcast_to(item_emb[:, None, :], ub.shape)
        att_in = jnp.concatenate([q, ub, q - ub, q * ub], axis=-1)
        h = att_in @ w_att1.T + b_att1
        score = (h @ w_att2.T + b_att2)[..., 0]
        score = jnp.where(mask, 0.0, score)
        browse = jnp.einsum('bl,ble->be', score, ub)
        feat = jnp.concatenate([item_emb, browse, user_emb], axis=-1)
        x = _dice(feat @ w1.T + b1, a1, g1, be1)
        x = _dice(x @ w2.T + b2, a2, g2, be2)
        x = jax.nn.sigmoid(x @ w3.T + b3)
        return x[:, 0]
    y = _L0_rec_ref(r_user, r_item, r_rec_his, L0_rec_table_user, L0_rec_table_i1, L0_rec_table_i2, L0_rec_table_i3, L0_rec_w_att1, L0_rec_b_att1, L0_rec_w_att2, L0_rec_b_att2, L0_rec_w1, L0_rec_b1, L0_rec_a1, L0_rec_g1, L0_rec_be1, L0_rec_w2, L0_rec_b2, L0_rec_a2, L0_rec_g2, L0_rec_be2, L0_rec_w3, L0_rec_b3)
    return y

_drawn_inputs = setup_inputs


def setup_inputs(seed=0):
    import zlib

    import numpy as np

    out = dict(_drawn_inputs(seed))
    spreads = {'L0_rec_b_att1': (0.0, 0.322),
     'L0_rec_b1': (0.0, 0.8),
     'L0_rec_g1': (1.0, 0.2),
     'L0_rec_be1': (0.0, 0.751),
     'L0_rec_b2': (0.0, 0.8),
     'L0_rec_g2': (1.0, 0.6),
     'L0_rec_be2': (0.0, 0.787)}
    factors = {'L0_rec_a1': 7.103, 'L0_rec_a2': 8.0}
    for name, (base, spread) in spreads.items():
        noise = np.random.default_rng([zlib.crc32(name.encode()), seed]).standard_normal(out[name].shape)
        drawn = base * np.exp(spread * noise) if base else spread * noise
        out[name] = jnp.asarray(drawn.astype(out[name].dtype))
    for name, factor in factors.items():
        out[name] = (out[name] * factor).astype(out[name].dtype)
    return out
```

```python
from contextlib import ExitStack

import concourse.bass as bass
from concourse import mybir

F32 = mybir.dt.float32
BF16 = mybir.dt.bfloat16
I32 = mybir.dt.int32
U32 = mybir.dt.uint32
ALU = mybir.AluOpType
ACT = mybir.ActivationFunctionType
AX = mybir.AxisListType

FEAT = (1, 2, 0)


def build(nc, r_user, r_item, r_his, table_user, table_i1, table_i2, table_i3, w_att1, b_att1,
          w_att2, b_att2, w1, b1, a1, g1, be1, w2, b2, a2, g2, be2, w3, b3, out):
    B, HIST, NF = r_his.shape
    V, D = table_i1.shape
    VU, DU = table_user.shape
    HID = w_att1.shape[0]
    H1, H2 = w1.shape[0], w2.shape[0]
    tables = (table_i1, table_i2, table_i3)
    E = NF * D
    EPS = 1e-8
    ROUND = 1.5 * 2.0 ** 23

    POS = HIST // 2
    HI, LO = 42, 24
    HJ, U = NF * HI, NF * LO
    TILE, HALF = 128, 64
    TILES = B // TILE
    STEPS = 16
    SLOTS = 32
    QUADS = HALF // 2
    MH = H1 // 2
    assert HI * LO >= V and HJ <= 128 and STEPS * 8 == TILE and 2 * POS == HIST
    FULL_HI = V // LO
    REST = V - FULL_HI * LO

    with ExitStack() as ctx:
        def sb(name, shape, dt=F32):
            return ctx.enter_context(nc.sbuf_tensor(name, shape, dt))

        def pb(name, shape, dt=F32):
            return ctx.enter_context(nc.psum_tensor(name, shape, dt))

        def sem(name):
            return ctx.enter_context(nc.semaphore(name))

        scoretab = sb("scoretab", [HJ, 2, HALF, U])
        weightsum = sb("weightsum", [TILE, U, TILE])
        onehot_hi = sb("onehot_hi", [POS, 4, 4, NF, HI, 4], BF16)
        onehot_lo = sb("onehot_lo", [POS, 4, 4, NF, LO, 4], BF16)
        scaled_lo = sb("scaled_lo", [POS, 2, 4, 3, U, 4], BF16)
        hiT = sb("hiT", [HJ, 2, 8, POS])
        picked = sb("picked", [POS, 2, 2, 4, U])
        score = sb("score", [POS, 2, 4, 4])
        score_m = sb("score_m", [POS, 4, 4])
        score_r = sb("score_r", [POS, 4, 4])
        parts = sb("parts", [POS, 2, 4, 3, 4], BF16)
        digits = sb("digits", [POS, 2, 2, QUADS, NF, 4], BF16)
        keep = sb("keep", [POS, 2, QUADS, 4])
        raw = sb("raw", [HALF, HIST * NF], I32)
        raw_f = sb("raw_f", [HALF, HIST * NF])
        digit_f = sb("digit_f", [HALF, HIST * NF])
        digits_b = sb("digits_b", [HALF, 2, HIST * NF], BF16)
        iota_i = sb("iota_i", [POS, HI, 4], I32)
        iota_hi = sb("iota_hi", [POS, HI, 4], BF16)
        iota_lo = sb("iota_lo", [POS, LO, 4], BF16)
        identf = sb("identf", [128, 128])
        identb = sb("identb", [128, 128], BF16)
        table_blk = sb("table_blk", [HJ, LO, NF, D])
        tableT = sb("tableT", [E + 1, LO, HJ])
        item_ids = sb("item_ids", [TILE, TILES, NF], I32)
        user_ids = sb("user_ids", [TILE, TILES], I32)
        ids_f = sb("ids_f", [TILE, TILES])
        ids_raw = sb("ids_raw", [TILE, TILES])
        ids_neg = sb("ids_neg", [TILE, TILES])
        ids_u = sb("ids_u", [TILE, TILES, NF + 1], U32)
        ids_now = sb("ids_now", [TILE, NF + 1], U32)
        item_rows = sb("item_rows", [TILE, NF, D])
        user_rows = sb("user_rows", [TILE, DU])
        item_now = sb("item_now", [E + 1, TILE])
        item_all = sb("item_all", [E, B])
        queryT = sb("queryT", [E + 1, TILE])
        mapq = sb("mapq", [E + 1, E + 1])
        vcol = sb("vcol", [E, 2])
        wa = sb("wa", [HID, 4, NF, D])
        wd = sb("wd", [HID + 1, E + 1])
        w2col = sb("w2col", [HID + 1, E + 1])
        browse = sb("browse", [TILE, E])
        browseT = sb("browseT", [E, TILE])
        userT = sb("userT", [DU, TILE])
        w1_rows = sb("w1_rows", [MH, 2, 2 * E + DU])
        w1T = sb("w1T", [E, 3, 2, MH])
        w2_rows = sb("w2_rows", [H2, H1])
        w2T = sb("w2T", [MH, 2, H2])
        w3T = sb("w3T", [H2, 1])
        par1 = sb("par1", [MH, 4, 2])
        par2 = sb("par2", [H2, 4])
        b3s = sb("b3s", [1, 1])
        x1 = sb("x1", [MH, 2, B])
        stats = sb("stats", [128, 3, 4, 6])
        mv = sb("mv", [128, 3, 2])
        dice = sb("dice", [128, 3, 8])
        probs = sb("probs", [1, B])
        tail1 = scoretab[0:MH, :, :, :].rearrange("p a b u -> p (a b u)")
        gate1 = tail1[:, 0:2 * B].rearrange("p (m b) -> p m b", m=2)
        norm1 = tail1[:, 2 * B:4 * B].rearrange("p (m b) -> p m b", m=2)
        tail2 = weightsum[0:H2, :, :].rearrange("p a b -> p (a b)")
        x2 = tail2[:, 0:B]
        gate2 = tail2[:, B:2 * B]
        norm2 = tail2[:, 2 * B:3 * B]

        sel = pb("sel", [128, 4, 512])
        hiT_ps = pb("hiT_ps", [128, 2, 1024], BF16)
        wsum_ps = pb("wsum_ps", [128, 512])
        misc = pb("misc", [128, 512])
        misc_b = misc[:, :].bitcast(BF16)

        weights_in = sem("weights_in")
        tables_in = sem("tables_in")
        small_in = sem("small_in")
        item_ids_in = sem("item_ids_in")
        user_ids_in = sem("user_ids_in")
        raw_in = sem("raw_in")
        item_rows_in = sem("item_rows_in")
        user_rows_in = sem("user_rows_in")
        blk_zero = sem("blk_zero")
        const_ready = sem("const_ready")
        pool_step = sem("pool_step")
        attw_ready = sem("attw_ready")
        vcol_ready = sem("vcol_ready")
        mapq_ready = sem("mapq_ready")
        ids_ready = sem("ids_ready")
        raw_f_ready = sem("raw_f_ready")
        digit_step = sem("digit_step")
        digits_b_ready = sem("digits_b_ready")
        keep_ready = sem("keep_ready")
        hi_ready = sem("hi_ready")
        lo_ready = sem("lo_ready")
        hiT_full = sem("hiT_full")
        hiT_copied = sem("hiT_copied")
        sel_full = sem("sel_full")
        picked_ready = sem("picked_ready")
        score_ready = sem("score_ready")
        split_step = sem("split_step")
        parts_ready = sem("parts_ready")
        scaled_ready = sem("scaled_ready")
        wsum_full = sem("wsum_full")
        wsum_copied = sem("wsum_copied")
        misc_full = sem("misc_full")
        misc_copied = sem("misc_copied")
        dve_tail = sem("dve_tail")
        dve_tail_pre = sem("dve_tail_pre")
        root_ready = sem("root_ready")
        y_ready = sem("y_ready")
        gate_ready = sem("gate_ready")
        head_full = sem("head_full")
        head_copied = sem("head_copied")
        pool_passed = sem("pool_passed")
        pe_passed = sem("pe_passed")
        out_done = sem("out_done")

        prologue = (["attw"] + [("tableT", i) for i in range(6)] + ["w1T", "w1uT", "w2T"]
                    + [("digit", 0, 0), ("digit", 1, 0), "item", "query"] + [("scoretab", r, 0) for r in range(9)])
        FIN = ["finish", "browseT", "userT", "layer1"]
        in_slot = {}
        for r in range(3):
            in_slot[r] = ("scoretab", r, 1)
        for i, name in enumerate(FIN):
            in_slot[3 + i] = name
        in_slot[7], in_slot[8] = ("digit", 0, 1), ("digit", 1, 1)
        for r in range(3, 9):
            in_slot[6 + r] = ("scoretab", r, 1)
        in_slot[16], in_slot[17] = "item", "query"
        for r in range(5):
            in_slot[18 + r] = ("scoretab", r, 0)
        in_slot[23], in_slot[24] = ("digit", 0, 0), ("digit", 1, 0)
        for r in range(5, 9):
            in_slot[20 + r] = ("scoretab", r, 0)
        order = sorted(in_slot)
        PER_TILE = len(order)

        def misc_before(t, slot):
            k = order.index(slot)
            if isinstance(t, int) and t == 0 and slot < 3:
                return len(prologue) + k
            return t * PER_TILE + (len(prologue) - len(FIN) + k)

        N_SMALL = 2 * NF + 1 + 3 + 8
        FIRST = 7
        SC_LAG = 3

        ctx.enter_context(nc.allow_non_contiguous_dma(reason="a few hundred weights and ids, loaded once"))
        block = ctx.enter_context(nc.Block())

        @block.sync
        def _(sp):
            his_rows = r_his.rearrange("b l f -> b (l f)")
            sp.dma_start(raw[:, :], his_rows[0:HALF, :]).then_inc(raw_in, 16)
            sp.dma_start(item_ids[:, :, :], r_item.rearrange("(t p) f -> p t f", p=TILE)).then_inc(item_ids_in, 16)
            wsrc = w_att1.rearrange("h (a f e) -> h a f e", a=4, f=NF)
            for j in range(NF):
                sp.dma_start(wa[:, :, j, :], wsrc[:, :, FEAT[j], :]).then_inc(weights_in, 16)
            sp.wait_ge(attw_ready, 1)
            sp.dma_start(w2col[0:HID, E:E + 1], w_att2.rearrange("o h -> h o")).then_inc(weights_in, 16)
            sp.dma_start(wd[0:HID, E:E + 1], b_att1.rearrange("(h o) -> h o", o=1)).then_inc(weights_in, 16)
            sp.dma_start(wd[HID:HID + 1, E:E + 1], b_att2.rearrange("(h o) -> h o", o=1)).then_inc(weights_in, 16)
            sp.wait_ge(blk_zero, 1)
            for j in range(NF):
                src = tables[FEAT[j]]
                sp.dma_start(table_blk[j * HI:j * HI + FULL_HI, :, j, :],
                             src[0:FULL_HI * LO, :].rearrange("(h l) e -> h l e", l=LO)).then_inc(tables_in, 16)
                sp.dma_start(table_blk[j * HI + FULL_HI:j * HI + FULL_HI + 1, 0:REST, j, :],
                             src[FULL_HI * LO:V, :].rearrange("(h l) e -> h l e", l=REST)).then_inc(tables_in, 16)
            with sp.Fori(1, 2 * TILES) as h:
                sp.wait_ge(raw_f_ready, h)
                sp.dma_start(raw[:, :], his_rows[bass.ds(h * HALF, HALF), :]).then_inc(raw_in, 16)
            sp.wait_ge(head_copied, 8)
            sp.dma_start(out.rearrange("(o b) -> o b", o=1), probs[:, :]).then_inc(out_done, 16)
            sp.wait_ge(out_done, 16)

        @block.gpsimd
        def _(pool):
            n_step = [0]

            def await_ge(signal, value):
                pool.wait_ge(signal, value)
                if not isinstance(value, int):
                    pool.sem_inc(pool_passed, 1)

            def chain(ins):
                n_step[0] += 1
                ins.then_inc(pool_step, 1)
                pool.wait_ge(pool_step, n_step[0])

            def make_digits(h):
                await_ge(raw_in, (h + 1) * 16)
                pool.tensor_copy(raw_f[:, :], raw[:, :]).then_inc(raw_f_ready, 1)
                await_ge(raw_f_ready, h + 1)
                pool.tensor_scalar(digit_f[:, :], raw_f[:, :], 1.0 / LO, -(LO - 1) / 2 / LO, ALU.mult, ALU.add
                                   ).then_inc(digit_step, 1)
                await_ge(digit_step, 2 * h + 1)
                pool.tensor_scalar(digit_f[:, :], digit_f[:, :], ROUND, None, ALU.add).then_inc(digit_step, 1)
                await_ge(digit_step, 2 * h + 2)
                pool.tensor_scalar(digits_b[:, 1, :], digit_f[:, :], -ROUND, float(LO), ALU.add, ALU.mult
                                   ).then_inc(digits_b_ready, 1)
                await_ge(digits_b_ready, 2 * h + 1)
                pool.tensor_tensor(digits_b[:, 0, :], raw_f[:, :], digits_b[:, 1, :], ALU.subtract
                                   ).then_inc(digits_b_ready, 1)

            def make_keep(n, hb):
                d = [digits[:, hb, k, :, NF - 1, :] for k in range(2)]
                pool.tensor_tensor(keep[:, hb, :, :], d[0], d[1], ALU.add).then_inc(keep_ready, 1)
                await_ge(keep_ready, 2 * n + 1)
                pool.tensor_scalar(keep[:, hb, :, :], keep[:, hb, :, :], 0.0, None, ALU.is_gt).then_inc(keep_ready, 1)

            def gather_items(t):
                pool.tensor_copy(ids_now[:, 0:NF], ids_u[:, bass.ds(t, 1), 0:NF].rearrange("p o f -> p (o f)")
                                 ).then_inc(ids_ready, 1)
                await_ge(ids_ready, 1 if isinstance(t, int) else 2 * t)
                for j in range(NF):
                    pool.indirect_dma_start(out=item_rows[:, j, :], out_offset=None, in_=tables[FEAT[j]],
                                            in_offset=bass.IndirectOffsetOnAxis(ap=ids_now[:, j:j + 1], axis=0)
                                            ).then_inc(item_rows_in, 16)

            def gather_users(t):
                pool.tensor_copy(ids_now[:, NF:NF + 1], ids_u[:, bass.ds(t, 1), NF:NF + 1].rearrange("p o f -> p (o f)")
                                 ).then_inc(ids_ready, 1)
                await_ge(ids_ready, 2 * TILES if isinstance(t, int) else 2 * t + 3)
                pool.indirect_dma_start(out=user_rows[:, :], out_offset=None, in_=table_user,
                                        in_offset=bass.IndirectOffsetOnAxis(ap=ids_now[:, NF:NF + 1], axis=0)
                                        ).then_inc(user_rows_in, 16)

            def split(t, n):
                k = t * STEPS + n
                hb, q0, p2 = n // 8, (n % 8) * 4, n % 2
                if n in (0, 8):
                    await_ge(keep_ready, (2 * t + hb + 1) * 2)
                pool.wait_ge(score_ready, 2 * k + 2)
                if not (isinstance(k, int) and k < 2):
                    pool.wait_ge(scaled_ready, k - 1)
                sc, kp = score[:, p2, :, :], keep[:, hb, q0:q0 + 4, :]
                pool.tensor_tensor(score_m[:, :, :], sc, kp, ALU.mult)
                pool.tensor_tensor(parts[:, p2, :, 0, :], sc, kp, ALU.mult).then_inc(split_step, 1)
                pool.wait_ge(split_step, 2 * k + 1)
                pool.tensor_tensor(score_r[:, :, :], score_m[:, :, :], parts[:, p2, :, 0, :], ALU.subtract)
                pool.tensor_tensor(parts[:, p2, :, 1, :], score_m[:, :, :], parts[:, p2, :, 0, :], ALU.subtract
                                   ).then_inc(split_step, 1)
                pool.wait_ge(split_step, 2 * k + 2)
                pool.tensor_tensor(parts[:, p2, :, 2, :], score_r[:, :, :], parts[:, p2, :, 1, :], ALU.subtract
                                   ).then_inc(parts_ready, 1)

            def step(t, n, last=False):
                split(t, n)
                if n == 0:
                    await_ge(misc_full, digit_read(t, 0))
                    make_digits(2 * t + 1)
                if n == 3 and not last:
                    await_ge(misc_full, item_read(t))
                    gather_items(t + 1)
                if n == 4:
                    if not (isinstance(t, int) and t == 0):
                        await_ge(misc_full, misc_before(t, 5) + 1)
                    gather_users(t)
                if n == 5:
                    await_ge(misc_copied, misc_before(t, 8) + 1)
                    make_keep(2 * t + 1, 1)
                if n == 8 and not last:
                    await_ge(misc_full, misc_before(t, 8) + 1)
                    make_digits(2 * t + 2)
                if n == 13 and not last:
                    await_ge(misc_copied, misc_before(t, 24) + 1)
                    make_keep(2 * t + 2, 0)

            def digit_read(t, _):
                return len(prologue) - 11 if isinstance(t, int) and t == 0 else misc_before(t - 1, 24) + 1

            def item_read(t):
                return len(prologue) - 10 if isinstance(t, int) and t == 0 else misc_before(t - 1, 16) + 1

            chain(pool.memset(identf[:, :], 0.0))
            chain(pool.affine_select(out=identf[:, :], in_=identf[:, :], compare_op=ALU.not_equal, fill=1.0,
                                     base=0, pattern=[[-1, 128]], channel_multiplier=1))
            pool.tensor_copy(identb[:, :], identf[:, :]).then_inc(const_ready, 1)
            chain(pool.iota(iota_i[:, :, :], pattern=[[LO, HI], [0, 4]], base=0, channel_multiplier=0))
            chain(pool.tensor_copy(iota_hi[:, :, :], iota_i[:, :, :]))
            chain(pool.iota(iota_i[:, 0:LO, :], pattern=[[1, LO], [0, 4]], base=0, channel_multiplier=0))
            pool.tensor_copy(iota_lo[:, :, :], iota_i[:, 0:LO, :]).then_inc(const_ready, 1)
            await_ge(item_ids_in, 16)
            for c in range(NF + 1):
                rows = V if c < NF else VU
                src = item_ids[:, :, FEAT[c]] if c < NF else user_ids[:, :]
                if c == NF:
                    await_ge(user_ids_in, 16)
                chain(pool.tensor_copy(ids_raw[:, :], src))
                chain(pool.tensor_scalar(ids_neg[:, :], ids_raw[:, :], 0.0, float(rows), ALU.is_lt, ALU.mult))
                chain(pool.tensor_tensor(ids_f[:, :], ids_raw[:, :], ids_neg[:, :], ALU.add))
                chain(pool.tensor_scalar(ids_u[:, :, c], ids_f[:, :], 0.0, float(rows - 1), ALU.max, ALU.min))
            make_digits(0)
            gather_items(0)
            await_ge(misc_copied, len(prologue) - 11)
            make_keep(0, 0)
            for n in range(2):
                step(0, n)
            with pool.Fori(0, TILES - 1) as t:
                for n in range(2, STEPS + 2):
                    step(t + n // STEPS, n % STEPS)
            for n in range(2, STEPS):
                step(TILES - 1, n, last=True)

        @block.tensor
        def _(pe):
            def await_ge(signal, value):
                pe.wait_ge(signal, value)
                if not isinstance(value, int):
                    pe.sem_inc(pe_passed, 1)

            def transpose_hi(t, s):
                k = t * SLOTS + s
                pe.wait_ge(hi_ready, t * STEPS + s // 2 + 1)
                if not (isinstance(k, int) and k < 2):
                    pe.wait_ge(hiT_copied, k - 1)
                for c in range(8):
                    q = (s % 2) * 2 + c // 4
                    mm = pe.transpose(hiT_ps[0:HJ, s % 2, c * POS:(c + 1) * POS],
                                      onehot_hi[:, (s // 2) % 4, q, :, :, c % 4].rearrange("p j h -> p (j h)"),
                                      identb[0:POS, 0:POS])
                mm.then_inc(hiT_full, 1)

            def read_scores(t, s):
                k = t * SLOTS + s
                pe.wait_ge(hiT_copied, k + 1)
                if s in (0, 16):
                    pe.wait_ge(misc_copied, scoretab_done(t, s // 16))
                if not (isinstance(k, int) and k < 2):
                    pe.wait_ge(picked_ready, k - 1)
                for c in range(8):
                    b = (s % 16) * 4 + c // 2
                    mm = pe.matmul(sel[0:POS, 2 * (s % 2) + c // 4, (c % 4) * U:(c % 4 + 1) * U],
                                   hiT[:, s % 2, c, :], scoretab[:, s // 16, b, :], start=True, stop=True)
                mm.then_inc(sel_full, 1)

            def scoretab_done(t, hb):
                if hb == 0:
                    return len(prologue) if isinstance(t, int) and t == 0 else misc_before(t - 1, 28) + 1
                return misc_before(t, 14) + 1

            def add_scores(t, s):
                k = t * SLOTS + s
                n = s // 2
                pe.wait_ge(scaled_ready, t * STEPS + n + 1)
                if not (isinstance(k, int) and k < 1):
                    pe.wait_ge(wsum_copied, k)
                for b in range(4):
                    q = (s % 2) * 2 + b // 2
                    for i in range(6):
                        c = (b % 2) * 2 + i // 3
                        mm = pe.matmul(wsum_ps[0:HJ, b * U:(b + 1) * U],
                                       onehot_hi[:, n % 4, q, :, :, c].rearrange("p j h -> p (j h)"),
                                       scaled_lo[:, n % 2, q, i % 3, :, c], start=(i == 0), stop=(i == 5))
                mm.then_inc(wsum_full, 1)

            def task(what, seq, t):
                if not (isinstance(seq, int) and seq < 1):
                    await_ge(misc_copied, seq)
                name = what if isinstance(what, str) else what[0]
                if name == "attw":
                    await_ge(attw_ready, 3)
                    pe.matmul(misc[0:E, 0:1], wa[:, 0, :, :].rearrange("p j e -> p (j e)"), w2col[0:HID, E:E + 1],
                              start=True, stop=True)
                    pe.matmul(misc[0:E, 1:2], wa[:, 3, :, :].rearrange("p j e -> p (j e)"), w2col[0:HID, E:E + 1],
                              start=True, stop=True)
                    mm = pe.matmul(misc[0:E + 1, 2:E + 3], w2col[:, :], wd[:, :], start=True, stop=True)
                elif name == "tableT":
                    await_ge(tables_in, 2 * NF * 16)
                    for i in range(4):
                        lo = what[1] * 4 + i
                        mm = pe.transpose(misc[0:E, i * HJ:(i + 1) * HJ],
                                          table_blk[:, lo, :, :].rearrange("p j e -> p (j e)"), identf[0:HJ, 0:HJ])
                elif name == "w1T":
                    await_ge(small_in, 16 * N_SMALL)
                    for m in range(2):
                        for g in range(2):
                            i = g * 2 + m
                            mm = pe.transpose(misc[0:E, i * MH:(i + 1) * MH], w1_rows[:, m, g * E:(g + 1) * E],
                                              identf[0:MH, 0:MH])
                elif name == "w1uT":
                    for m in range(2):
                        mm = pe.transpose(misc[0:DU, m * MH:(m + 1) * MH], w1_rows[:, m, 2 * E:2 * E + DU],
                                          identf[0:MH, 0:MH])
                elif name == "w2T":
                    for m in range(2):
                        mm = pe.transpose(misc[0:MH, m * H2:(m + 1) * H2], w2_rows[:, m * MH:(m + 1) * MH],
                                          identf[0:H2, 0:H2])
                elif name == "digit":
                    hb, kind = what[2], what[1]
                    await_ge(digits_b_ready, (t * 2 + hb) * 2 + 2)
                    src = digits_b[:, kind, :].rearrange("p (c l f) -> p f c l", c=2, f=NF)
                    for j in range(NF):
                        for c in range(2):
                            i = j * 2 + c
                            mm = pe.transpose(misc_b[0:POS, i * HALF:(i + 1) * HALF], src[:, FEAT[j], c, :],
                                              identb[0:HALF, 0:HALF])
                elif name == "item":
                    await_ge(item_rows_in, (t + 1) * (NF * 16))
                    mm = pe.transpose(misc[0:E, 0:TILE], item_rows[:, :, :].rearrange("p j e -> p (j e)"),
                                      identf[:, :])
                elif name == "query":
                    if isinstance(t, int) and t == 0:
                        await_ge(mapq_ready, 1)
                    mm = pe.matmul(misc[0:E + 1, 0:TILE], mapq[:, :], item_now[:, :], start=True, stop=True)
                elif name == "scoretab":
                    r, hb = what[1], what[2]
                    j = r // 3
                    rows = slice(j * D, (j + 1) * D) if j < NF - 1 else slice(j * D, E + 1)
                    for i in range(8):
                        lo = (r % 3) * 8 + i
                        mm = pe.matmul(misc[0:HJ, i * HALF:(i + 1) * HALF], tableT[rows, lo, :],
                                       queryT[rows, hb * HALF:(hb + 1) * HALF], start=True, stop=True)
                elif name == "finish":
                    await_ge(wsum_copied, (t + 1) * SLOTS)
                    for j in range(NF):
                        for lo in range(LO):
                            mm = pe.matmul(misc[:, j * D:(j + 1) * D], weightsum[0:HJ, j * LO + lo, :],
                                           table_blk[:, lo, j, :], start=(lo == 0), stop=(lo == LO - 1))
                elif name == "browseT":
                    mm = pe.transpose(misc[0:E, 0:TILE], browse[:, :], identf[:, :])
                elif name == "userT":
                    await_ge(user_rows_in, (t + 1) * 16)
                    mm = pe.transpose(misc[0:DU, 0:TILE], user_rows[:, :], identf[:, :])
                elif name == "layer1":
                    for m in range(2):
                        o = misc[0:MH, m * TILE:(m + 1) * TILE]
                        pe.matmul(o, w1T[:, 0, m, :], item_all[:, bass.ds(t * TILE, TILE)], start=True, stop=False)
                        pe.matmul(o, w1T[:, 1, m, :], browseT[:, :], start=False, stop=False)
                        mm = pe.matmul(o, w1T[0:DU, 2, m, :], userT[:, :], start=False, stop=True)
                mm.then_inc(misc_full, 1)

            def slot(t, s, last=False):
                if s < SLOTS - 1:
                    transpose_hi(t, s + 1)
                elif not last:
                    transpose_hi(t + 1, 0)
                read_scores(t, s)
                if s in in_slot:
                    what = in_slot[s]
                    if what in FIN:
                        if not (isinstance(t, int) and t == 0):
                            task(what, misc_before(t, s), t - 1)
                    elif s < 16:
                        task(what, misc_before(t, s), t)
                    elif not last:
                        task(what, misc_before(t, s), t + 1)
                if s >= SC_LAG:
                    add_scores(t, s - SC_LAG)
                elif not (isinstance(t, int) and t == 0):
                    add_scores(t - 1, s - SC_LAG + SLOTS)

            pe.wait_ge(const_ready, 1)
            for seq, what in enumerate(prologue):
                task(what, seq, 0)
            transpose_hi(0, 0)
            for s in range(FIRST):
                slot(0, s)
            with pe.Fori(0, TILES - 1) as t:
                for s in range(FIRST, SLOTS + FIRST):
                    slot(t + s // SLOTS, s % SLOTS)
            for s in range(FIRST, SLOTS):
                slot(TILES - 1, s, last=True)
            for s in range(SLOTS - SC_LAG, SLOTS):
                add_scores(TILES - 1, s)
            base = misc_before(TILES - 1, 14) + 1
            for i, what in enumerate(FIN):
                task(what, base + i, TILES - 1)
            for q in range(4):
                pe.wait_ge(y_ready, 2 * q + 2)
                for m in range(2):
                    mm = pe.matmul(sel[0:H2, q, :], w2T[:, m, :], norm1[:, m, q * 512:(q + 1) * 512],
                                   start=(m == 0), stop=(m == 1))
                mm.then_inc(head_full, 1)
            for q in range(4):
                pe.wait_ge(y_ready, 8 + q + 1)
                pe.wait_ge(head_copied, 4)
                pe.matmul(sel[0:1, q, :], w3T[:, :], norm2[:, q * 512:(q + 1) * 512],
                          start=True, stop=True).then_inc(head_full, 1)

        @block.scalar
        def _(act):
            act.dma_start(user_ids[:, :], r_user.rearrange("(t p) o -> p (t o)", p=TILE)).then_inc(user_ids_in, 16)
            n_small = 0
            for g in range(2):
                for j in range(NF):
                    act.dma_start(w1_rows[:, :, g * E + j * D:g * E + (j + 1) * D],
                                  w1.rearrange("(m p) k -> p m k", m=2)[:, :, g * E + FEAT[j] * D:g * E + (FEAT[j] + 1) * D]
                                  ).then_inc(small_in, 16)
                    n_small += 1
            act.dma_start(w1_rows[:, :, 2 * E:2 * E + DU], w1.rearrange("(m p) k -> p m k", m=2)[:, :, 2 * E:2 * E + DU]
                          ).then_inc(small_in, 16)
            act.dma_start(w2_rows[:, :], w2).then_inc(small_in, 16)
            act.dma_start(w3T[:, :], w3.rearrange("o h -> h o")).then_inc(small_in, 16)
            act.dma_start(b3s[:, :], b3.rearrange("(o h) -> o h", o=1)).then_inc(small_in, 16)
            n_small += 4
            for i, v in enumerate((b1, a1, g1, be1)):
                act.dma_start(par1[:, i, :], v.rearrange("(m p) -> p m", m=2)).then_inc(small_in, 16)
                n_small += 1
            for i, v in enumerate((b2, a2, g2, be2)):
                act.dma_start(par2[:, i:i + 1], v.rearrange("(p o) -> p o", o=1)).then_inc(small_in, 16)
                n_small += 1
            assert n_small == N_SMALL

            def copy_hiT(t, s):
                k = t * SLOTS + s
                act.wait_ge(hiT_full, k + 1)
                if not (isinstance(k, int) and k < 2):
                    act.wait_ge(sel_full, k - 1)
                act.activation(hiT[:, s % 2, :, :].rearrange("p c l -> p (c l)"), hiT_ps[0:HJ, s % 2, 0:8 * POS],
                               ACT.Copy).then_inc(hiT_copied, 1)

            def copy_sums(t, s):
                act.wait_ge(wsum_full, t * SLOTS + s + 1)
                act.activation(weightsum[0:HJ, :, 4 * s:4 * s + 4].rearrange("p u b -> p b u"),
                               wsum_ps[0:HJ, 0:4 * U].rearrange("p (b u) -> p b u", b=4), ACT.Copy
                               ).then_inc(wsum_copied, 1)

            def task(what, seq, t):
                act.wait_ge(misc_full, seq + 1)
                name = what if isinstance(what, str) else what[0]
                if name == "attw":
                    act.activation(vcol[:, :], misc[0:E, 0:2], ACT.Copy).then_inc(vcol_ready, 1)
                    act.activation(mapq[0:E, E:E + 1], misc[0:E, 0:1], ACT.Copy)
                    ins = act.activation(mapq[E:E + 1, :], misc[E:E + 1, 2:E + 3], ACT.Copy)
                elif name == "tableT":
                    i = what[1]
                    ins = act.activation(tableT[0:E, 4 * i:4 * i + 4, :].rearrange("p l h -> p (l h)"),
                                         misc[0:E, 0:4 * HJ], ACT.Copy)
                elif name == "w1T":
                    ins = act.activation(w1T[:, 0:2, :, :].rearrange("p g m h -> p (g m h)"), misc[0:E, 0:4 * MH], ACT.Copy)
                elif name == "w1uT":
                    ins = act.activation(w1T[0:DU, 2, :, :].rearrange("p m h -> p (m h)"), misc[0:DU, 0:2 * MH], ACT.Copy)
                elif name == "w2T":
                    ins = act.activation(w2T[:, :, :].rearrange("p m h -> p (m h)"), misc[0:MH, 0:2 * H2], ACT.Copy)
                elif name == "digit":
                    kind, hb = what[1], what[2]
                    for j in range(NF):
                        ins = act.activation(
                            digits[:, hb, kind, :, j, :].rearrange("p q (b c) -> p c q b", c=2),
                            misc_b[0:POS, 2 * j * HALF:(2 * j + 2) * HALF].rearrange("p (c q b) -> p c q b", c=2, b=2),
                            ACT.Copy)
                elif name == "item":
                    act.activation(item_now[0:E, :], misc[0:E, 0:TILE], ACT.Copy)
                    ins = act.activation(item_all[:, bass.ds(t * TILE, TILE)], misc[0:E, 0:TILE], ACT.Copy)
                elif name == "query":
                    ins = act.activation(queryT[:, :], misc[0:E + 1, 0:TILE], ACT.Copy)
                elif name == "scoretab":
                    r, hb = what[1], what[2]
                    ins = act.activation(scoretab[:, hb, :, 8 * r:8 * r + 8].rearrange("p b u -> p u b"),
                                         misc[0:HJ, :].rearrange("p (u b) -> p u b", u=8), ACT.Copy)
                elif name == "finish":
                    ins = act.activation(browse[:, :], misc[:, 0:E], ACT.Copy)
                elif name == "browseT":
                    ins = act.activation(browseT[:, :], misc[0:E, 0:TILE], ACT.Copy)
                elif name == "userT":
                    ins = act.activation(userT[:, :], misc[0:DU, 0:TILE], ACT.Copy)
                elif name == "layer1":
                    for m in range(2):
                        ins = act.activation(x1[:, m, bass.ds(t * TILE, TILE)], misc[0:MH, m * TILE:(m + 1) * TILE],
                                             ACT.Identity, bias=par1[:, 0, m:m + 1])
                ins.then_inc(misc_copied, 1)

            def slot(t, s, last=False):
                if s < SLOTS - 1:
                    copy_hiT(t, s + 1)
                elif not last:
                    copy_hiT(t + 1, 0)
                if s in in_slot:
                    what = in_slot[s]
                    if what in FIN:
                        if not (isinstance(t, int) and t == 0):
                            task(what, misc_before(t, s), t - 1)
                    elif s < 16:
                        task(what, misc_before(t, s), t)
                    elif not last:
                        task(what, misc_before(t, s), t + 1)
                if s >= SC_LAG:
                    copy_sums(t, s - SC_LAG)
                elif not (isinstance(t, int) and t == 0):
                    copy_sums(t - 1, s - SC_LAG + SLOTS)

            act.wait_ge(blk_zero, 2)
            for seq, what in enumerate(prologue):
                task(what, seq, 0)
            act.wait_ge(small_in, 16 * N_SMALL)
            copy_hiT(0, 0)
            for s in range(FIRST):
                slot(0, s)
            with act.Fori(0, TILES - 1) as t:
                for s in range(FIRST, SLOTS + FIRST):
                    slot(t + s // SLOTS, s % SLOTS)
            for s in range(FIRST, SLOTS):
                slot(TILES - 1, s, last=True)
            for s in range(SLOTS - SC_LAG, SLOTS):
                copy_sums(TILES - 1, s)
            base = misc_before(TILES - 1, 14) + 1
            for i, what in enumerate(FIN):
                task(what, base + i, TILES - 1)

            act.wait_ge(dve_tail, 1)
            act.activation(dice[0:MH, 0:2, 1], dice[0:MH, 0:2, 0], ACT.Sqrt).then_inc(root_ready, 1)
            act.wait_ge(dve_tail, 2)
            for q in range(4):
                for m in range(2):
                    c = slice(q * 512, (q + 1) * 512)
                    act.activation(gate1[:, m, c], x1[:, m, c], ACT.Sigmoid, bias=dice[0:MH, m, 4:5],
                                   scale=dice[0:MH, m, 3:4])
                    act.activation(norm1[:, m, c], x1[:, m, c], ACT.Identity, bias=dice[0:MH, m, 4:5],
                                   scale=dice[0:MH, m, 3:4]).then_inc(gate_ready, 1)
            for q in range(4):
                act.wait_ge(head_full, q + 1)
                act.activation(x2[:, q * 512:(q + 1) * 512], sel[0:H2, q, :], ACT.Identity,
                               bias=par2[:, 0:1]).then_inc(head_copied, 1)
            act.wait_ge(dve_tail, 3)
            act.activation(dice[0:H2, 2:3, 1], dice[0:H2, 2:3, 0], ACT.Sqrt).then_inc(root_ready, 1)
            act.wait_ge(dve_tail, 4)
            for q in range(4):
                c = slice(q * 512, (q + 1) * 512)
                act.activation(gate2[:, c], x2[:, c], ACT.Sigmoid, bias=dice[0:H2, 2, 4:5], scale=dice[0:H2, 2, 3:4])
                act.activation(norm2[:, c], x2[:, c], ACT.Identity, bias=dice[0:H2, 2, 4:5],
                               scale=dice[0:H2, 2, 3:4]).then_inc(gate_ready, 1)
            for q in range(4):
                act.wait_ge(head_full, 4 + q + 1)
                act.activation(probs[:, q * 512:(q + 1) * 512], sel[0:1, q, :], ACT.Sigmoid,
                               bias=b3s[:, :]).then_inc(head_copied, 1)

        @block.vector
        def _(dve):
            def onehots(t, n):
                k = t * STEPS + n
                hb, q0, s4 = n // 8, (n % 8) * 4, n % 4
                if n in (0, 8):
                    if isinstance(t, int) and t == 0 and n == 0:
                        dve.wait_ge(misc_copied, len(prologue) - 11)
                    elif n == 0:
                        dve.wait_ge(misc_copied, misc_before(t - 1, 24) + 1)
                    else:
                        dve.wait_ge(misc_copied, misc_before(t, 8) + 1)
                if not (isinstance(k, int) and k < 4):
                    dve.wait_ge(wsum_full, 2 * k - 6)
                for kind, dst, iota, size, done in ((1, onehot_hi, iota_hi, HI, hi_ready), (0, onehot_lo, iota_lo, LO, lo_ready)):
                    src = digits[:, hb, kind, q0:q0 + 4, :, :].rearrange("p q j c -> p (q j) c")
                    dve.tensor_tensor(dst[:, s4, :, :, :, :].rearrange("p q j v c -> p (q j) v c"),
                                      src.unsqueeze(2).to_broadcast([POS, 4 * NF, size, 4]),
                                      iota[:, :, :].unsqueeze(1).to_broadcast([POS, 4 * NF, size, 4]),
                                      ALU.is_equal).then_inc(done, 1)

            def pick(t, s):
                k = t * SLOTS + s
                n = s // 2
                q0 = (s % 2) * 2
                dve.wait_ge(sel_full, k + 1)
                dve.wait_ge(lo_ready, t * STEPS + n + 1)
                dve.tensor_tensor(picked[:, s % 2, :, :, :],
                                  sel[0:POS, 2 * (s % 2):2 * (s % 2) + 2, 0:4 * U].rearrange("p q (c u) -> p q c u", c=4),
                                  onehot_lo[:, n % 4, q0:q0 + 2, :, :, :].rearrange("p q j v c -> p q c (j v)"),
                                  ALU.mult).then_inc(picked_ready, 1)
                dve.wait_ge(picked_ready, k + 1)
                dve.tensor_reduce(score[:, n % 2, q0:q0 + 2, :].rearrange("p q c -> p (q c)"),
                                  picked[:, s % 2, :, :, :].rearrange("p q c u -> p (q c) u"), AX.X, ALU.add
                                  ).then_inc(score_ready, 1)

            def scale(t, n):
                k = t * STEPS + n
                dve.wait_ge(parts_ready, k + 1)
                if not (isinstance(k, int) and k < 2):
                    dve.wait_ge(wsum_full, 2 * k - 2)
                for q in range(4):
                    ins = dve.tensor_tensor(
                        scaled_lo[:, n % 2, q, :, :, :],
                        onehot_lo[:, n % 4, q, :, :, :].rearrange("p j v c -> p (j v) c").unsqueeze(1)
                        .to_broadcast([POS, 3, U, 4]),
                        parts[:, n % 2, q, :, :].unsqueeze(2).to_broadcast([POS, 3, U, 4]), ALU.mult)
                ins.then_inc(scaled_ready, 1)

            def step(t, n, last=False):
                pick(t, 2 * n)
                pick(t, 2 * n + 1)
                if n < STEPS - 2:
                    onehots(t, n + 2)
                elif not last:
                    onehots(t + 1, n + 2 - STEPS)
                scale(t, n)

            dve.memset(w2col[:, :], 0.0).then_inc(dve_tail_pre, 1)
            dve.memset(wd[:, :], 0.0).then_inc(dve_tail_pre, 1)
            dve.wait_ge(dve_tail_pre, 2)
            dve.memset(w2col[:, E:E + 1], 1.0).then_inc(attw_ready, 1)
            dve.memset(table_blk[:, :, :, :], 0.0).then_inc(blk_zero, 1)
            dve.memset(tableT[E:E + 1, :, :], 0.0).then_inc(dve_tail_pre, 1)
            dve.memset(item_now[E:E + 1, :], 1.0)
            dve.wait_ge(dve_tail_pre, 3)
            dve.memset(tableT[E:E + 1, :, (NF - 1) * HI:NF * HI], 1.0).then_inc(blk_zero, 1)
            dve.wait_ge(weights_in, (NF + 3) * 16)
            flat = [wa[:, a, :, :].rearrange("p j e -> p (j e)") for a in range(4)]
            dve.tensor_tensor(wd[0:HID, 0:E], flat[1], flat[2], ALU.subtract).then_inc(attw_ready, 1)
            dve.tensor_tensor(flat[0], flat[0], flat[2], ALU.add).then_inc(attw_ready, 1)
            dve.wait_ge(vcol_ready, 1)
            dve.wait_ge(const_ready, 1)
            dve.tensor_scalar(mapq[0:E, 0:E], identf[0:E, 0:E], vcol[:, 1:2], None, ALU.mult).then_inc(mapq_ready, 1)
            dve.wait_ge(const_ready, 2)

            onehots(0, 0)
            onehots(0, 1)
            for n in range(2):
                step(0, n)
            with dve.Fori(0, TILES - 1) as t:
                for n in range(2, STEPS + 2):
                    step(t + n // STEPS, n % STEPS)
            for n in range(2, STEPS):
                step(TILES - 1, n, last=True)

            tail_n = [3]

            def chain(ins):
                tail_n[0] += 1
                ins.then_inc(dve_tail_pre, 1)
                dve.wait_ge(dve_tail_pre, tail_n[0])

            def moments(x, rows, m0, m1, stage):
                for m in range(m0, m1):
                    for q in range(4):
                        ins = dve.bn_stats(stats[0:rows, m, q, :], x(m)[:, q * 512:(q + 1) * 512])
                chain(ins)
                for m in range(m0, m1):
                    ins = dve.bn_aggr(mv[0:rows, m, :], stats[0:rows, m, :, :].rearrange("p q s -> p (q s)"))
                chain(ins)
                dve.tensor_scalar(dice[0:rows, m0:m1, 0], mv[0:rows, m0:m1, 1], float(B) / (B - 1), EPS,
                                  ALU.mult, ALU.add).then_inc(dve_tail, 1)

            def affine(rows, m0, m1, gamma, beta, alpha):
                d = dice[0:rows, m0:m1, :]
                dve.tensor_scalar(d[:, :, 5], alpha, -1.0, 1.0, ALU.mult, ALU.add)
                chain(dve.reciprocal(d[:, :, 2], d[:, :, 1]))
                chain(dve.tensor_tensor(d[:, :, 3], d[:, :, 2], gamma, ALU.mult))
                chain(dve.tensor_tensor(d[:, :, 6], mv[0:rows, m0:m1, 0], d[:, :, 3], ALU.mult))
                dve.tensor_tensor(d[:, :, 4], beta, d[:, :, 6], ALU.subtract).then_inc(dve_tail, 1)

            dve.wait_ge(misc_copied, misc_before(TILES - 1, 14) + 1 + len(FIN))
            moments(lambda m: x1[:, m, :], MH, 0, 2, 0)
            dve.wait_ge(root_ready, 1)
            affine(MH, 0, 2, par1[:, 2, :], par1[:, 3, :], par1[:, 1, :])
            for q in range(4):
                for m in range(2):
                    c = slice(q * 512, (q + 1) * 512)
                    dve.wait_ge(gate_ready, 2 * q + m + 1)
                    chain(dve.tensor_scalar(gate1[:, m, c], gate1[:, m, c], dice[0:MH, m, 5:6], par1[:, 1, m:m + 1],
                                            ALU.mult, ALU.add))
                    dve.tensor_tensor(norm1[:, m, c], norm1[:, m, c], gate1[:, m, c], ALU.mult).then_inc(y_ready, 1)
            dve.wait_ge(head_copied, 4)
            moments(lambda m: x2, H2, 2, 3, 1)
            dve.wait_ge(root_ready, 2)
            affine(H2, 2, 3, par2[:, 2:3], par2[:, 3:4], par2[:, 1:2])
            for q in range(4):
                c = slice(q * 512, (q + 1) * 512)
                dve.wait_ge(gate_ready, 8 + q + 1)
                chain(dve.tensor_scalar(gate2[:, c], gate2[:, c], dice[0:H2, 2, 5:6], par2[:, 1:2], ALU.mult, ALU.add))
                dve.tensor_tensor(norm2[:, c], norm2[:, c], gate2[:, c], ALU.mult).then_inc(y_ready, 1)


_INS = ['r_user', 'r_item', 'r_rec_his', 'L0_rec_table_user', 'L0_rec_table_i1', 'L0_rec_table_i2',
        'L0_rec_table_i3', 'L0_rec_w_att1', 'L0_rec_b_att1', 'L0_rec_w_att2', 'L0_rec_b_att2', 'L0_rec_w1',
        'L0_rec_b1', 'L0_rec_a1', 'L0_rec_g1', 'L0_rec_be1', 'L0_rec_w2', 'L0_rec_b2', 'L0_rec_a2',
        'L0_rec_g2', 'L0_rec_be2', 'L0_rec_w3', 'L0_rec_b3']


def kernel(**inputs):
    import numpy as np
    import concourse.bacc as bacc
    from concourse.bass_utils import run_bass_kernel_spmd

    nc = bacc.Bacc("TRN2", target_bir_lowering=False, num_devices=1)
    arrays, args = {}, []
    for name in _INS:
        a = np.ascontiguousarray(inputs[name])
        arrays[f"in_{name}_dram"] = a
        args.append(nc.dram_tensor(f"in_{name}_dram", a.shape, mybir.dt.from_np(a.dtype), kind="ExternalInput").ap())
    rows = inputs["r_user"].shape[0]
    out = nc.dram_tensor("out_0_dram", (rows,), F32, kind="ExternalOutput").ap()
    build(nc, *args, out)
    r = run_bass_kernel_spmd(nc, [arrays], core_ids=[0])
    return r.results[0]["out_0_dram"]
```

```python
from contextlib import ExitStack

import concourse.bass as bass
from concourse import mybir

F32 = mybir.dt.float32
BF16 = mybir.dt.bfloat16
I32 = mybir.dt.int32
U32 = mybir.dt.uint32
ALU = mybir.AluOpType
ACT = mybir.ActivationFunctionType
AX = mybir.AxisListType

FEAT = (1, 2, 0)


def build(nc, r_user, r_item, r_his, table_user, table_i1, table_i2, table_i3, w_att1, b_att1,
          w_att2, b_att2, w1, b1, a1, g1, be1, w2, b2, a2, g2, be2, w3, b3, out):
    B, HIST, NF = r_his.shape
    V, D = table_i1.shape
    VU, DU = table_user.shape
    HID = w_att1.shape[0]
    H1, H2 = w1.shape[0], w2.shape[0]
    tables = (table_i1, table_i2, table_i3)
    E = NF * D
    EPS = 1e-8
    ROUND = 1.5 * 2.0 ** 23

    POS = HIST // 2
    HI, LO = 42, 24
    HJ, U = NF * HI, NF * LO
    TILE, HALF = 128, 64
    TILES = B // TILE
    STEPS = 16
    SLOTS = 32
    QUADS = HALF // 2
    MH = H1 // 2
    assert HI * LO >= V and HJ <= 128 and STEPS * 8 == TILE and 2 * POS == HIST
    FULL_HI = V // LO
    REST = V - FULL_HI * LO

    with ExitStack() as ctx:
        def sb(name, shape, dt=F32):
            return ctx.enter_context(nc.sbuf_tensor(name, shape, dt))

        def pb(name, shape, dt=F32):
            return ctx.enter_context(nc.psum_tensor(name, shape, dt))

        def sem(name):
            return ctx.enter_context(nc.semaphore(name))

        scoretab = sb("scoretab", [128, 2, HALF // 4, 3, U, 4], BF16)
        scores_f = sb("scores_f", [HJ, HALF // 4, LO, 4])
        scores_b = sb("scores_b", [HJ, HALF // 4, 3, LO, 4], BF16)
        wsum_ring = sb("wsum_ring", [128, 2, U, TILE // 4])
        weightsum = sb("weightsum", [128, 4, LO, TILE // 4])
        onehot_hi = sb("onehot_hi", [POS, 4, 4 * HJ * 4 + 8], BF16)
        onehot_lo = sb("onehot_lo", [POS, 4, 4, NF, LO, 4], BF16)
        scaled_lo = sb("scaled_lo", [POS, 2, 4, 3, U, 4], BF16)
        hiT = sb("hiT", [128, 2, 8 * POS + 128 - POS], BF16)
        picked = sb("picked", [POS, 2, 2, 4, U])
        score = sb("score", [POS, 2, 4, 4])
        score_m = sb("score_m", [POS, 4, 4])
        score_r = sb("score_r", [POS, 4, 4])
        parts = sb("parts", [POS, 2, 4, 3, 4], BF16)
        digits = sb("digits", [POS, 2, 2, QUADS, NF, 4], BF16)
        keep = sb("keep", [POS, 2, QUADS, 4])
        raw = sb("raw", [HALF, HIST * NF], I32)
        raw_f = sb("raw_f", [HALF, HIST * NF])
        digit_f = raw[:, :].bitcast(F32)
        digits_b = sb("digits_b", [HALF, 2, HIST * NF], BF16)
        iota_i = sb("iota_i", [POS, HI, 4], I32)
        iota_hi = sb("iota_hi", [POS, HI, 4], BF16)
        iota_lo = sb("iota_lo", [POS, LO, 4], BF16)
        identf = sb("identf", [128, 128])
        identb = sb("identb", [128, 128], BF16)
        table_blk = sb("table_blk", [HJ, LO, NF, D])
        tableT = sb("tableT", [E + 1, LO, HJ])
        item_ids = sb("item_ids", [TILE, TILES, NF], I32)
        user_ids = sb("user_ids", [TILE, TILES], I32)
        ids_f = sb("ids_f", [TILE, TILES])
        ids_raw = sb("ids_raw", [TILE, TILES])
        ids_neg = sb("ids_neg", [TILE, TILES])
        ids_u = sb("ids_u", [TILE, TILES, NF + 1], U32)
        ids_now = sb("ids_now", [TILE, NF + 1], U32)
        item_rows = sb("item_rows", [TILE, NF, D])
        user_rows = sb("user_rows", [TILE, DU])
        item_now = sb("item_now", [E + 1, TILE])
        item_last = sb("item_last", [E, TILE])
        queryT = sb("queryT", [E + 1, TILE])
        mapq = sb("mapq", [E + 1, E + 1])
        vcol = sb("vcol", [E, 2])
        wa = sb("wa", [HID, 4, NF, D])
        wd = sb("wd", [HID + 1, E + 1])
        w2col = sb("w2col", [HID + 1, E + 1])
        browseT = sb("browseT", [E, TILE])
        userT = sb("userT", [DU, TILE])
        weights_flat = weightsum[:, :, :, :].rearrange("p w l b -> p (w l b)")
        w1_rows = weights_flat[0:MH, 0:2 * (2 * E + DU)].rearrange("p (m k) -> p m k", m=2)
        w1T = sb("w1T", [E, 3, 2, MH])
        w2_rows = weights_flat[0:H2, 1024:1024 + H1]
        w2T = sb("w2T", [MH, 2, H2])
        w3T = sb("w3T", [H2, 1])
        par1 = sb("par1", [MH, 4, 2])
        par2 = sb("par2", [H2, 4])
        b3s = sb("b3s", [1, 1])
        x1 = sb("x1", [MH, 2, B])
        stats = sb("stats", [128, 3, 4, 6])
        mv = sb("mv", [128, 3, 2])
        dice = sb("dice", [128, 3, 8])
        probs = table_blk[0:1, :, :, :].rearrange("p l j e -> p (l j e)")[:, 0:B]
        tail1 = scoretab[0:MH, :, :, :, :, :].rearrange("p a b c d e -> p (a b c d e)").bitcast(F32)
        gate1 = tail1[:, 0:2 * B].rearrange("p (m b) -> p m b", m=2)
        norm1 = tail1[:, 2 * B:4 * B].rearrange("p (m b) -> p m b", m=2)
        tail2 = wsum_ring[0:H2, :, :, :].rearrange("p a u b -> p (a u b)")
        x2, gate2 = tail2[:, 0:B], tail2[:, B:2 * B]
        norm2 = weightsum[0:H2, :, :, :].rearrange("p a l b -> p (a l b)")[:, 0:B]

        sel = pb("sel", [128, 4, 512])
        hiT_ps = pb("hiT_ps", [128, 2, 1024], BF16)
        wsum_ps = pb("wsum_ps", [128, 512])
        misc = pb("misc", [128, 512])
        misc_b = misc[:, :].bitcast(BF16)

        weights_in = sem("weights_in")
        tables_in = sem("tables_in")
        small_in = sem("small_in")
        item_ids_in = sem("item_ids_in")
        user_ids_in = sem("user_ids_in")
        raw_in = sem("raw_in")
        item_rows_in = sem("item_rows_in")
        user_rows_in = sem("user_rows_in")
        blk_zero = sem("blk_zero")
        const_ready = sem("const_ready")
        pool_step = sem("pool_step")
        attw_ready = sem("attw_ready")
        vcol_ready = sem("vcol_ready")
        mapq_ready = sem("mapq_ready")
        ids_ready = sem("ids_ready")
        raw_f_ready = sem("raw_f_ready")
        digit_step = sem("digit_step")
        digits_b_ready = sem("digits_b_ready")
        keep_ready = sem("keep_ready")
        hi_ready = sem("hi_ready")
        lo_ready = sem("lo_ready")
        hiT_full = sem("hiT_full")
        hiT_copied = sem("hiT_copied")
        sel_full = sem("sel_full")
        picked_ready = sem("picked_ready")
        score_ready = sem("score_ready")
        split_step = sem("split_step")
        parts_ready = sem("parts_ready")
        scaled_ready = sem("scaled_ready")
        wsum_full = sem("wsum_full")
        wsum_copied = sem("wsum_copied")
        scoretab_zero = sem("scoretab_zero")
        scores_split = sem("scores_split")
        scores_step = sem("scores_step")
        scoretab_in = sem("scoretab_in")
        weightsum_in = sem("weightsum_in")
        misc_full = sem("misc_full")
        misc_copied = sem("misc_copied")
        dve_tail = sem("dve_tail")
        dve_tail_pre = sem("dve_tail_pre")
        root_ready = sem("root_ready")
        y_ready = sem("y_ready")
        gate_ready = sem("gate_ready")
        head_full = sem("head_full")
        head_copied = sem("head_copied")
        pool_passed = sem("pool_passed")
        pe_passed = sem("pe_passed")
        sp_passed = sem("sp_passed")
        item_kept = sem("item_kept")
        out_done = sem("out_done")

        prologue = (["attw"] + [("tableT", i) for i in range(6)] + ["w1T", "w1uT", "w2T"]
                    + [("digit", 0, 0), ("digit", 1, 0), "item", "query"] + [("scoretab", r, 0) for r in range(3)])
        DIGITS0 = prologue.index(("digit", 1, 0)) + 1
        ITEM0 = prologue.index("item") + 1
        FIN = ["userT", "finish", "layer1"]
        in_slot = {0: ("scoretab", 0, 1), 1: ("scoretab", 1, 1), 2: ("scoretab", 2, 1),
                   4: "userT", 5: "finish", 6: "layer1", 7: ("digit", 0, 1), 8: ("digit", 1, 1),
                   16: "item", 17: "query", 18: ("scoretab", 0, 0), 19: ("scoretab", 1, 0), 20: ("scoretab", 2, 0),
                   23: ("digit", 0, 0), 24: ("digit", 1, 0)}
        order = sorted(in_slot)
        PER_TILE = len(order)

        def misc_before(t, slot):
            k = order.index(slot)
            if isinstance(t, int) and t == 0 and slot < 3:
                return len(prologue) + k
            return t * PER_TILE + (len(prologue) - len(FIN) + k)

        N_SMALL = 2 * NF + 1 + 3 + 8
        FIRST = 7
        SC_LAG = 3

        ctx.enter_context(nc.allow_non_contiguous_dma(reason="a few hundred weights and ids, loaded once"))
        block = ctx.enter_context(nc.Block())

        @block.sync
        def _(sp):
            def await_ge(signal, value):
                sp.wait_ge(signal, value)
                if not isinstance(value, int):
                    sp.sem_inc(sp_passed, 1)

            his_rows = r_his.rearrange("b l f -> b (l f)")
            sp.dma_start(raw[:, :], his_rows[0:HALF, :]).then_inc(raw_in, 16)
            sp.dma_start(item_ids[:, :, :], r_item.rearrange("(t p) f -> p t f", p=TILE)).then_inc(item_ids_in, 16)
            wsrc = w_att1.rearrange("h (a f e) -> h a f e", a=4, f=NF)
            for j in range(NF):
                sp.dma_start(wa[:, :, j, :], wsrc[:, :, FEAT[j], :]).then_inc(weights_in, 16)
            sp.wait_ge(attw_ready, 1)
            sp.dma_start(w2col[0:HID, E:E + 1], w_att2.rearrange("o h -> h o")).then_inc(weights_in, 16)
            sp.dma_start(wd[0:HID, E:E + 1], b_att1.rearrange("(h o) -> h o", o=1)).then_inc(weights_in, 16)
            sp.dma_start(wd[HID:HID + 1, E:E + 1], b_att2.rearrange("(h o) -> h o", o=1)).then_inc(weights_in, 16)
            sp.wait_ge(blk_zero, 1)
            for j in range(NF):
                src = tables[FEAT[j]]
                sp.dma_start(table_blk[j * HI:j * HI + FULL_HI, :, j, :],
                             src[0:FULL_HI * LO, :].rearrange("(h l) e -> h l e", l=LO)).then_inc(tables_in, 16)
                sp.dma_start(table_blk[j * HI + FULL_HI:j * HI + FULL_HI + 1, 0:REST, j, :],
                             src[FULL_HI * LO:V, :].rearrange("(h l) e -> h l e", l=REST)).then_inc(tables_in, 16)

            def load_rows(h):
                await_ge(digits_b_ready, 2 * h)
                sp.dma_start(raw[:, :], his_rows[bass.ds(h * HALF, HALF), :]).then_inc(raw_in, 16)

            def place_scores(t, hb):
                g = 2 * t + hb
                await_ge(scores_split, 3 * g + 3)
                if isinstance(g, int) and g < 2:
                    sp.wait_ge(scoretab_zero, hb + 1)
                else:
                    await_ge(sel_full, 16 * g - 16)
                for j in range(NF):
                    r = slice(j * HI, (j + 1) * HI)
                    sp.dma_start(scoretab[r, hb, :, :, j * LO:(j + 1) * LO, :].rearrange("p q k l b -> p (q k) (l b)"),
                                 scores_b[r, :, :, :, :].rearrange("p q k l b -> p (q k) (l b)")
                                 ).then_inc(scoretab_in, 16)

            def collect_sums(t, w):
                k = 4 * t + w
                await_ge(wsum_copied, 8 * k + 8)
                if not (isinstance(k, int) and k < 1):
                    await_ge(weightsum_in, NF * 16 * k)
                if w == 0 and not (isinstance(t, int) and t == 0):
                    await_ge(misc_full, misc_before(t, 5) + 1)
                for j in range(NF):
                    r = slice(j * HI, (j + 1) * HI)
                    sp.dma_start(weightsum[r, w, :, :].rearrange("p l b -> p (l b)"),
                                 wsum_ring[r, w % 2, j * LO:(j + 1) * LO, :].rearrange("p l b -> p (l b)")
                                 ).then_inc(weightsum_in, 16)

            def tile(t, last=False):
                load_rows(2 * t + 1)
                if not (isinstance(t, int) and t == 0):
                    collect_sums(t - 1, 3)
                place_scores(t, 1)
                collect_sums(t, 0)
                if not last:
                    load_rows(2 * t + 2)
                collect_sums(t, 1)
                if not last:
                    place_scores(t + 1, 0)
                collect_sums(t, 2)

            place_scores(0, 0)
            tile(0)
            with sp.Fori(1, TILES - 1) as t:
                tile(t)
            tile(TILES - 1, last=True)
            collect_sums(TILES - 1, 3)
            sp.wait_ge(head_copied, 8)
            sp.dma_start(out.rearrange("(o b) -> o b", o=1), probs).then_inc(out_done, 16)
            sp.wait_ge(out_done, 16)

        @block.gpsimd
        def _(pool):
            n_step = [0]

            def await_ge(signal, value):
                pool.wait_ge(signal, value)
                if not isinstance(value, int):
                    pool.sem_inc(pool_passed, 1)

            def chain(ins):
                n_step[0] += 1
                ins.then_inc(pool_step, 1)
                pool.wait_ge(pool_step, n_step[0])

            def make_digits(h):
                await_ge(raw_in, (h + 1) * 16)
                pool.tensor_copy(raw_f[:, :], raw[:, :]).then_inc(raw_f_ready, 1)
                await_ge(raw_f_ready, h + 1)
                pool.tensor_scalar(digit_f, raw_f[:, :], 1.0 / LO, -(LO - 1) / 2 / LO, ALU.mult, ALU.add
                                   ).then_inc(digit_step, 1)
                await_ge(digit_step, 2 * h + 1)
                pool.tensor_scalar(digit_f, digit_f, ROUND, None, ALU.add).then_inc(digit_step, 1)
                await_ge(digit_step, 2 * h + 2)
                pool.tensor_scalar(digits_b[:, 1, :], digit_f, -ROUND, float(LO), ALU.add, ALU.mult
                                   ).then_inc(digits_b_ready, 1)
                await_ge(digits_b_ready, 2 * h + 1)
                pool.tensor_tensor(digits_b[:, 0, :], raw_f[:, :], digits_b[:, 1, :], ALU.subtract
                                   ).then_inc(digits_b_ready, 1)

            def make_keep(n, hb):
                d = [digits[:, hb, k, :, NF - 1, :] for k in range(2)]
                pool.tensor_tensor(keep[:, hb, :, :], d[0], d[1], ALU.add).then_inc(keep_ready, 1)
                await_ge(keep_ready, 2 * n + 1)
                pool.tensor_scalar(keep[:, hb, :, :], keep[:, hb, :, :], 0.0, None, ALU.is_gt).then_inc(keep_ready, 1)

            def gather_items(t):
                pool.tensor_copy(ids_now[:, 0:NF], ids_u[:, bass.ds(t, 1), 0:NF].rearrange("p o f -> p (o f)")
                                 ).then_inc(ids_ready, 1)
                await_ge(ids_ready, 1 if isinstance(t, int) else 2 * t)
                for j in range(NF):
                    pool.indirect_dma_start(out=item_rows[:, j, :], out_offset=None, in_=tables[FEAT[j]],
                                            in_offset=bass.IndirectOffsetOnAxis(ap=ids_now[:, j:j + 1], axis=0)
                                            ).then_inc(item_rows_in, 16)

            def gather_users(t):
                pool.tensor_copy(ids_now[:, NF:NF + 1], ids_u[:, bass.ds(t, 1), NF:NF + 1].rearrange("p o f -> p (o f)")
                                 ).then_inc(ids_ready, 1)
                await_ge(ids_ready, 2 * TILES if isinstance(t, int) else 2 * t + 3)
                pool.indirect_dma_start(out=user_rows[:, :], out_offset=None, in_=table_user,
                                        in_offset=bass.IndirectOffsetOnAxis(ap=ids_now[:, NF:NF + 1], axis=0)
                                        ).then_inc(user_rows_in, 16)

            def split(t, n):
                k = t * STEPS + n
                hb, q0, p2 = n // 8, (n % 8) * 4, n % 2
                if n in (0, 8):
                    await_ge(keep_ready, (2 * t + hb + 1) * 2)
                pool.wait_ge(score_ready, 2 * k + 2)
                if not (isinstance(k, int) and k < 2):
                    pool.wait_ge(scaled_ready, k - 1)
                sc, kp = score[:, p2, :, :], keep[:, hb, q0:q0 + 4, :]
                pool.tensor_tensor(score_m[:, :, :], sc, kp, ALU.mult)
                pool.tensor_tensor(parts[:, p2, :, 0, :], sc, kp, ALU.mult).then_inc(split_step, 1)
                pool.wait_ge(split_step, 2 * k + 1)
                pool.tensor_tensor(score_r[:, :, :], score_m[:, :, :], parts[:, p2, :, 0, :], ALU.subtract)
                pool.tensor_tensor(parts[:, p2, :, 1, :], score_m[:, :, :], parts[:, p2, :, 0, :], ALU.subtract
                                   ).then_inc(split_step, 1)
                pool.wait_ge(split_step, 2 * k + 2)
                pool.tensor_tensor(parts[:, p2, :, 2, :], score_r[:, :, :], parts[:, p2, :, 1, :], ALU.subtract
                                   ).then_inc(parts_ready, 1)

            def split_scores(copied, g, r):
                k = 3 * g + r
                lo = slice(8 * r, 8 * r + 8)
                full, part = scores_f[:, :, lo, :], [scores_b[:, :, i, lo, :] for i in range(3)]
                await_ge(misc_copied, copied)
                pool.tensor_tensor(part[1], full, part[0], ALU.subtract).then_inc(scores_step, 1)
                await_ge(scores_step, 2 * k + 1)
                pool.tensor_tensor(full, full, part[0], ALU.subtract).then_inc(scores_step, 1)
                await_ge(scores_step, 2 * k + 2)
                pool.tensor_tensor(part[2], full, part[1], ALU.subtract).then_inc(scores_split, 1)

            def step(t, n, last=False):
                split(t, n)
                if n in (1, 2, 3):
                    split_scores(misc_before(t, n - 1) + 1, 2 * t + 1, n - 1)
                if n in (10, 11, 12) and not last:
                    split_scores(misc_before(t, n + 8) + 1, 2 * t + 2, n - 10)
                if n == 0:
                    await_ge(misc_full, digit_read(t, 0))
                    make_digits(2 * t + 1)
                if n == 3 and not last:
                    await_ge(misc_full, item_read(t))
                    gather_items(t + 1)
                if n == 4:
                    if not (isinstance(t, int) and t == 0):
                        await_ge(misc_full, misc_before(t, 4) + 1)
                    gather_users(t)
                if n == 5:
                    await_ge(misc_copied, misc_before(t, 8) + 1)
                    make_keep(2 * t + 1, 1)
                if n == 8 and not last:
                    await_ge(misc_full, misc_before(t, 8) + 1)
                    make_digits(2 * t + 2)
                if n == 13 and not last:
                    await_ge(misc_copied, misc_before(t, 24) + 1)
                    make_keep(2 * t + 2, 0)

            def digit_read(t, _):
                return DIGITS0 if isinstance(t, int) and t == 0 else misc_before(t - 1, 24) + 1

            def item_read(t):
                return ITEM0 if isinstance(t, int) and t == 0 else misc_before(t - 1, 16) + 1

            chain(pool.memset(identf[:, :], 0.0))
            chain(pool.affine_select(out=identf[:, :], in_=identf[:, :], compare_op=ALU.not_equal, fill=1.0,
                                     base=0, pattern=[[-1, 128]], channel_multiplier=1))
            pool.tensor_copy(identb[:, :], identf[:, :]).then_inc(const_ready, 1)
            chain(pool.iota(iota_i[:, :, :], pattern=[[LO, HI], [0, 4]], base=0, channel_multiplier=0))
            chain(pool.tensor_copy(iota_hi[:, :, :], iota_i[:, :, :]))
            chain(pool.iota(iota_i[:, 0:LO, :], pattern=[[1, LO], [0, 4]], base=0, channel_multiplier=0))
            pool.tensor_copy(iota_lo[:, :, :], iota_i[:, 0:LO, :]).then_inc(const_ready, 1)
            await_ge(item_ids_in, 16)
            for c in range(NF + 1):
                rows = V if c < NF else VU
                src = item_ids[:, :, FEAT[c]] if c < NF else user_ids[:, :]
                if c == NF:
                    await_ge(user_ids_in, 16)
                chain(pool.tensor_copy(ids_raw[:, :], src))
                chain(pool.tensor_scalar(ids_neg[:, :], ids_raw[:, :], 0.0, float(rows), ALU.is_lt, ALU.mult))
                chain(pool.tensor_tensor(ids_f[:, :], ids_raw[:, :], ids_neg[:, :], ALU.add))
                chain(pool.tensor_scalar(ids_u[:, :, c], ids_f[:, :], 0.0, float(rows - 1), ALU.max, ALU.min))
            make_digits(0)
            gather_items(0)
            await_ge(misc_copied, DIGITS0)
            make_keep(0, 0)
            for r in range(3):
                split_scores(len(prologue) - 2 + r, 0, r)
            for n in range(2):
                step(0, n)
            with pool.Fori(0, TILES - 1) as t:
                for n in range(2, STEPS + 2):
                    step(t + n // STEPS, n % STEPS)
            for n in range(2, STEPS):
                step(TILES - 1, n, last=True)

        @block.tensor
        def _(pe):
            def await_ge(signal, value):
                pe.wait_ge(signal, value)
                if not isinstance(value, int):
                    pe.sem_inc(pe_passed, 1)

            def hi_columns(s4, q, c):
                return onehot_hi[:, s4, q * HJ * 4 + c:q * HJ * 4 + c + 127 * 4 + 1:4]

            def transpose_hi(t, s):
                k = t * SLOTS + s
                pe.wait_ge(hi_ready, t * STEPS + s // 2 + 1)
                if not (isinstance(k, int) and k < 2):
                    pe.wait_ge(hiT_copied, k - 1)
                for c in range(8):
                    q = (s % 2) * 2 + c // 4
                    mm = pe.transpose(hiT_ps[:, s % 2, c * POS:(c + 1) * POS], hi_columns((s // 2) % 4, q, c % 4),
                                      identb[0:POS, 0:POS])
                mm.then_inc(hiT_full, 1)

            def read_scores(t, s):
                k = t * SLOTS + s
                pe.wait_ge(hiT_copied, k + 1)
                if s in (0, 16):
                    pe.wait_ge(scoretab_in, (2 * t + s // 16 + 1) * (NF * 16))
                if not (isinstance(k, int) and k < 2):
                    pe.wait_ge(picked_ready, k - 1)
                for c in range(8):
                    b = (s % 16) * 4 + c // 2
                    for i in range(3):
                        mm = pe.matmul(sel[:, 2 * (s % 2) + c // 4, (c % 4) * U:(c % 4 + 1) * U],
                                       hiT[0:HJ, s % 2, c * POS:c * POS + 128],
                                       scoretab[0:HJ, s // 16, b // 4, i, :, b % 4], start=(i == 0), stop=(i == 2))
                mm.then_inc(sel_full, 1)

            def add_scores(t, s):
                k = t * SLOTS + s
                n = s // 2
                pe.wait_ge(scaled_ready, t * STEPS + n + 1)
                if not (isinstance(k, int) and k < 1):
                    pe.wait_ge(wsum_copied, k)
                for b in range(4):
                    q = (s % 2) * 2 + b // 2
                    for i in range(6):
                        c = (b % 2) * 2 + i // 3
                        mm = pe.matmul(wsum_ps[:, b * U:(b + 1) * U], hi_columns(n % 4, q, c),
                                       scaled_lo[:, n % 2, q, i % 3, :, c], start=(i == 0), stop=(i == 5))
                mm.then_inc(wsum_full, 1)

            def task(what, seq, t):
                if not (isinstance(seq, int) and seq < 1):
                    await_ge(misc_copied, seq)
                name = what if isinstance(what, str) else what[0]
                if name == "attw":
                    await_ge(attw_ready, 3)
                    pe.matmul(misc[0:E, 0:1], wa[:, 0, :, :].rearrange("p j e -> p (j e)"), w2col[0:HID, E:E + 1],
                              start=True, stop=True)
                    pe.matmul(misc[0:E, 1:2], wa[:, 3, :, :].rearrange("p j e -> p (j e)"), w2col[0:HID, E:E + 1],
                              start=True, stop=True)
                    mm = pe.matmul(misc[0:E + 1, 2:E + 3], w2col[:, :], wd[:, :], start=True, stop=True)
                elif name == "tableT":
                    await_ge(tables_in, 2 * NF * 16)
                    for i in range(4):
                        lo = what[1] * 4 + i
                        mm = pe.transpose(misc[0:E, i * HJ:(i + 1) * HJ],
                                          table_blk[:, lo, :, :].rearrange("p j e -> p (j e)"), identf[0:HJ, 0:HJ])
                elif name == "w1T":
                    await_ge(small_in, 16 * N_SMALL)
                    for m in range(2):
                        for g in range(2):
                            i = g * 2 + m
                            mm = pe.transpose(misc[0:E, i * MH:(i + 1) * MH], w1_rows[:, m, g * E:(g + 1) * E],
                                              identf[0:MH, 0:MH])
                elif name == "w1uT":
                    for m in range(2):
                        mm = pe.transpose(misc[0:DU, m * MH:(m + 1) * MH], w1_rows[:, m, 2 * E:2 * E + DU],
                                          identf[0:MH, 0:MH])
                elif name == "w2T":
                    for m in range(2):
                        mm = pe.transpose(misc[0:MH, m * H2:(m + 1) * H2], w2_rows[:, m * MH:(m + 1) * MH],
                                          identf[0:H2, 0:H2])
                elif name == "digit":
                    hb, kind = what[2], what[1]
                    await_ge(digits_b_ready, (t * 2 + hb) * 2 + 2)
                    src = digits_b[:, kind, :].rearrange("p (c l f) -> p f c l", c=2, f=NF)
                    for j in range(NF):
                        for c in range(2):
                            i = j * 2 + c
                            mm = pe.transpose(misc_b[0:POS, i * HALF:(i + 1) * HALF], src[:, FEAT[j], c, :],
                                              identb[0:HALF, 0:HALF])
                elif name == "item":
                    await_ge(item_rows_in, (t + 1) * (NF * 16))
                    mm = pe.transpose(misc[0:E, 0:TILE], item_rows[:, :, :].rearrange("p j e -> p (j e)"),
                                      identf[:, :])
                elif name == "query":
                    if isinstance(t, int) and t == 0:
                        await_ge(mapq_ready, 1)
                    mm = pe.matmul(misc[0:E + 1, 0:TILE], mapq[:, :], item_now[:, :], start=True, stop=True)
                elif name == "scoretab":
                    r, hb = what[1], what[2]
                    for i in range(8):
                        mm = pe.matmul(misc[0:HJ, i * HALF:(i + 1) * HALF], tableT[:, 8 * r + i, :],
                                       queryT[:, hb * HALF:(hb + 1) * HALF], start=True, stop=True)
                elif name == "finish":
                    await_ge(weightsum_in, (t + 1) * (4 * NF * 16))
                    for lo in range(LO):
                        mm = pe.matmul(misc[0:E, 0:TILE].rearrange("p (w b) -> p w b", w=4),
                                       table_blk[:, lo, :, :].rearrange("p j e -> p (j e)"),
                                       weightsum[0:HJ, :, lo, :], start=(lo == 0), stop=(lo == LO - 1))
                elif name == "userT":
                    await_ge(user_rows_in, (t + 1) * 16)
                    mm = pe.transpose(misc[0:DU, 0:TILE], user_rows[:, :], identf[:, :])
                elif name == "layer1":
                    items = item_now[0:E, :] if isinstance(t, int) and t == TILES - 1 else item_last[:, :]
                    for m in range(2):
                        o = misc[0:MH, m * TILE:(m + 1) * TILE]
                        pe.matmul(o, w1T[:, 0, m, :], items, start=True, stop=False)
                        pe.matmul(o, w1T[:, 1, m, :], browseT[:, :], start=False, stop=False)
                        mm = pe.matmul(o, w1T[0:DU, 2, m, :], userT[:, :], start=False, stop=True)
                mm.then_inc(misc_full, 1)

            def slot(t, s, last=False):
                if s < SLOTS - 1:
                    transpose_hi(t, s + 1)
                elif not last:
                    transpose_hi(t + 1, 0)
                read_scores(t, s)
                if s in in_slot:
                    what = in_slot[s]
                    if what in FIN:
                        if not (isinstance(t, int) and t == 0):
                            task(what, misc_before(t, s), t - 1)
                    elif s < 16:
                        task(what, misc_before(t, s), t)
                    elif not last:
                        task(what, misc_before(t, s), t + 1)
                if s >= SC_LAG:
                    add_scores(t, s - SC_LAG)
                elif not (isinstance(t, int) and t == 0):
                    add_scores(t - 1, s - SC_LAG + SLOTS)

            pe.wait_ge(const_ready, 1)
            for seq, what in enumerate(prologue):
                task(what, seq, 0)
            transpose_hi(0, 0)
            for s in range(FIRST):
                slot(0, s)
            with pe.Fori(0, TILES - 1) as t:
                for s in range(FIRST, SLOTS + FIRST):
                    slot(t + s // SLOTS, s % SLOTS)
            for s in range(FIRST, SLOTS):
                slot(TILES - 1, s, last=True)
            for s in range(SLOTS - SC_LAG, SLOTS):
                add_scores(TILES - 1, s)
            base = misc_before(TILES - 1, 8) + 1
            for i, what in enumerate(FIN):
                task(what, base + i, TILES - 1)
            for q in range(4):
                pe.wait_ge(y_ready, 2 * q + 2)
                for m in range(2):
                    mm = pe.matmul(sel[0:H2, q, :], w2T[:, m, :], norm1[:, m, q * 512:(q + 1) * 512],
                                   start=(m == 0), stop=(m == 1))
                mm.then_inc(head_full, 1)
            for q in range(4):
                pe.wait_ge(y_ready, 8 + q + 1)
                pe.wait_ge(head_copied, 4)
                pe.matmul(sel[0:1, q, :], w3T[:, :], norm2[:, q * 512:(q + 1) * 512],
                          start=True, stop=True).then_inc(head_full, 1)

        @block.scalar
        def _(act):
            act.dma_start(user_ids[:, :], r_user.rearrange("(t p) o -> p (t o)", p=TILE)).then_inc(user_ids_in, 16)
            n_small = 0
            for g in range(2):
                for j in range(NF):
                    act.dma_start(w1_rows[:, :, g * E + j * D:g * E + (j + 1) * D],
                                  w1.rearrange("(m p) k -> p m k", m=2)[:, :, g * E + FEAT[j] * D:g * E + (FEAT[j] + 1) * D]
                                  ).then_inc(small_in, 16)
                    n_small += 1
            act.dma_start(w1_rows[:, :, 2 * E:2 * E + DU], w1.rearrange("(m p) k -> p m k", m=2)[:, :, 2 * E:2 * E + DU]
                          ).then_inc(small_in, 16)
            act.dma_start(w2_rows, w2).then_inc(small_in, 16)
            act.dma_start(w3T[:, :], w3.rearrange("o h -> h o")).then_inc(small_in, 16)
            act.dma_start(b3s[:, :], b3.rearrange("(o h) -> o h", o=1)).then_inc(small_in, 16)
            n_small += 4
            for i, v in enumerate((b1, a1, g1, be1)):
                act.dma_start(par1[:, i, :], v.rearrange("(m p) -> p m", m=2)).then_inc(small_in, 16)
                n_small += 1
            for i, v in enumerate((b2, a2, g2, be2)):
                act.dma_start(par2[:, i:i + 1], v.rearrange("(p o) -> p o", o=1)).then_inc(small_in, 16)
                n_small += 1
            assert n_small == N_SMALL

            def copy_hiT(t, s):
                k = t * SLOTS + s
                act.wait_ge(hiT_full, k + 1)
                if not (isinstance(k, int) and k < 2):
                    act.wait_ge(sel_full, k - 1)
                act.activation(hiT[:, s % 2, 0:8 * POS], hiT_ps[:, s % 2, 0:8 * POS],
                               ACT.Copy).then_inc(hiT_copied, 1)

            def copy_sums(t, s):
                act.wait_ge(wsum_full, t * SLOTS + s + 1)
                k = t * 4 + s // 8
                if s % 8 == 0 and not (isinstance(k, int) and k < 2):
                    act.wait_ge(weightsum_in, NF * 16 * (k - 1))
                act.activation(wsum_ring[:, (s // 8) % 2, :, 4 * (s % 8):4 * (s % 8) + 4].rearrange("p u b -> p b u"),
                               wsum_ps[:, 0:4 * U].rearrange("p (b u) -> p b u", b=4), ACT.Copy
                               ).then_inc(wsum_copied, 1)

            def task(what, seq, t):
                act.wait_ge(misc_full, seq + 1)
                name = what if isinstance(what, str) else what[0]
                if name == "attw":
                    act.activation(vcol[:, :], misc[0:E, 0:2], ACT.Copy).then_inc(vcol_ready, 1)
                    act.activation(mapq[0:E, E:E + 1], misc[0:E, 0:1], ACT.Copy)
                    ins = act.activation(mapq[E:E + 1, :], misc[E:E + 1, 2:E + 3], ACT.Copy)
                elif name == "tableT":
                    i = what[1]
                    ins = act.activation(tableT[0:E, 4 * i:4 * i + 4, :].rearrange("p l h -> p (l h)"),
                                         misc[0:E, 0:4 * HJ], ACT.Copy)
                elif name == "w1T":
                    ins = act.activation(w1T[:, 0:2, :, :].rearrange("p g m h -> p (g m h)"), misc[0:E, 0:4 * MH], ACT.Copy)
                elif name == "w1uT":
                    ins = act.activation(w1T[0:DU, 2, :, :].rearrange("p m h -> p (m h)"), misc[0:DU, 0:2 * MH], ACT.Copy)
                elif name == "w2T":
                    ins = act.activation(w2T[:, :, :].rearrange("p m h -> p (m h)"), misc[0:MH, 0:2 * H2], ACT.Copy)
                elif name == "digit":
                    kind, hb = what[1], what[2]
                    for j in range(NF):
                        ins = act.activation(
                            digits[:, hb, kind, :, j, :].rearrange("p q (b c) -> p c q b", c=2),
                            misc_b[0:POS, 2 * j * HALF:(2 * j + 2) * HALF].rearrange("p (c q b) -> p c q b", c=2, b=2),
                            ACT.Copy)
                elif name == "item":
                    if not (isinstance(t, int) and t == 0):
                        act.activation(item_last[:, :], item_now[0:E, :], ACT.Copy).then_inc(item_kept, 1)
                        act.wait_ge(item_kept, t)
                    ins = act.activation(item_now[0:E, :], misc[0:E, 0:TILE], ACT.Copy)
                elif name == "query":
                    ins = act.activation(queryT[:, :], misc[0:E + 1, 0:TILE], ACT.Copy)
                elif name == "scoretab":
                    r, hb = what[1], what[2]
                    if r == 0 and not (isinstance(t, int) and t == 0 and hb == 0):
                        act.wait_ge(scoretab_in, (2 * t + hb) * (NF * 16))
                    src = misc[0:HJ, :].rearrange("p (l q b) -> p l q b", l=8, b=4)
                    act.activation(scores_f[:, :, 8 * r:8 * r + 8, :].rearrange("p q l b -> p l q b"), src, ACT.Copy)
                    ins = act.activation(scores_b[:, :, 0, 8 * r:8 * r + 8, :].rearrange("p q l b -> p l q b"), src,
                                         ACT.Copy)
                elif name == "finish":
                    ins = act.activation(browseT[:, :], misc[0:E, 0:TILE], ACT.Copy)
                elif name == "userT":
                    ins = act.activation(userT[:, :], misc[0:DU, 0:TILE], ACT.Copy)
                elif name == "layer1":
                    for m in range(2):
                        ins = act.activation(x1[:, m, bass.ds(t * TILE, TILE)], misc[0:MH, m * TILE:(m + 1) * TILE],
                                             ACT.Identity, bias=par1[:, 0, m:m + 1])
                ins.then_inc(misc_copied, 1)

            def slot(t, s, last=False):
                if s < SLOTS - 1:
                    copy_hiT(t, s + 1)
                elif not last:
                    copy_hiT(t + 1, 0)
                if s in in_slot:
                    what = in_slot[s]
                    if what in FIN:
                        if not (isinstance(t, int) and t == 0):
                            task(what, misc_before(t, s), t - 1)
                    elif s < 16:
                        task(what, misc_before(t, s), t)
                    elif not last:
                        task(what, misc_before(t, s), t + 1)
                if s >= SC_LAG:
                    copy_sums(t, s - SC_LAG)
                elif not (isinstance(t, int) and t == 0):
                    copy_sums(t - 1, s - SC_LAG + SLOTS)

            act.wait_ge(blk_zero, 2)
            for seq, what in enumerate(prologue):
                task(what, seq, 0)
            act.wait_ge(small_in, 16 * N_SMALL)
            copy_hiT(0, 0)
            for s in range(FIRST):
                slot(0, s)
            with act.Fori(0, TILES - 1) as t:
                for s in range(FIRST, SLOTS + FIRST):
                    slot(t + s // SLOTS, s % SLOTS)
            for s in range(FIRST, SLOTS):
                slot(TILES - 1, s, last=True)
            for s in range(SLOTS - SC_LAG, SLOTS):
                copy_sums(TILES - 1, s)
            base = misc_before(TILES - 1, 8) + 1
            for i, what in enumerate(FIN):
                task(what, base + i, TILES - 1)

            act.wait_ge(dve_tail, 1)
            act.activation(dice[0:MH, 0:2, 1], dice[0:MH, 0:2, 0], ACT.Sqrt).then_inc(root_ready, 1)
            act.wait_ge(dve_tail, 2)
            for q in range(4):
                for m in range(2):
                    c = slice(q * 512, (q + 1) * 512)
                    act.activation(gate1[:, m, c], x1[:, m, c], ACT.Sigmoid, bias=dice[0:MH, m, 4:5],
                                   scale=dice[0:MH, m, 3:4])
                    act.activation(norm1[:, m, c], x1[:, m, c], ACT.Identity, bias=dice[0:MH, m, 4:5],
                                   scale=dice[0:MH, m, 3:4]).then_inc(gate_ready, 1)
            for q in range(4):
                act.wait_ge(head_full, q + 1)
                act.activation(x2[:, q * 512:(q + 1) * 512], sel[0:H2, q, :], ACT.Identity,
                               bias=par2[:, 0:1]).then_inc(head_copied, 1)
            act.wait_ge(dve_tail, 3)
            act.activation(dice[0:H2, 2:3, 1], dice[0:H2, 2:3, 0], ACT.Sqrt).then_inc(root_ready, 1)
            act.wait_ge(dve_tail, 4)
            for q in range(4):
                c = slice(q * 512, (q + 1) * 512)
                act.activation(gate2[:, c], x2[:, c], ACT.Sigmoid, bias=dice[0:H2, 2, 4:5], scale=dice[0:H2, 2, 3:4])
                act.activation(norm2[:, c], x2[:, c], ACT.Identity, bias=dice[0:H2, 2, 4:5],
                               scale=dice[0:H2, 2, 3:4]).then_inc(gate_ready, 1)
            for q in range(4):
                act.wait_ge(head_full, 4 + q + 1)
                act.activation(probs[:, q * 512:(q + 1) * 512], sel[0:1, q, :], ACT.Sigmoid,
                               bias=b3s[:, :]).then_inc(head_copied, 1)

        @block.vector
        def _(dve):
            def onehots(t, n):
                k = t * STEPS + n
                hb, q0, s4 = n // 8, (n % 8) * 4, n % 4
                if n in (0, 8):
                    if isinstance(t, int) and t == 0 and n == 0:
                        dve.wait_ge(misc_copied, DIGITS0)
                    elif n == 0:
                        dve.wait_ge(misc_copied, misc_before(t - 1, 24) + 1)
                    else:
                        dve.wait_ge(misc_copied, misc_before(t, 8) + 1)
                if not (isinstance(k, int) and k < 4):
                    dve.wait_ge(wsum_full, 2 * k - 6)
                for kind, dst, iota, size, done in (
                        (1, onehot_hi[:, s4, 0:4 * HJ * 4].rearrange("p (q v c) -> p q v c", v=HI, c=4), iota_hi, HI, hi_ready),
                        (0, onehot_lo[:, s4, :, :, :, :].rearrange("p q j v c -> p (q j) v c"), iota_lo, LO, lo_ready)):
                    src = digits[:, hb, kind, q0:q0 + 4, :, :].rearrange("p q j c -> p (q j) c")
                    dve.tensor_tensor(dst,
                                      src.unsqueeze(2).to_broadcast([POS, 4 * NF, size, 4]),
                                      iota[:, :, :].unsqueeze(1).to_broadcast([POS, 4 * NF, size, 4]),
                                      ALU.is_equal).then_inc(done, 1)

            def pick(t, s):
                k = t * SLOTS + s
                n = s // 2
                q0 = (s % 2) * 2
                dve.wait_ge(sel_full, k + 1)
                dve.wait_ge(lo_ready, t * STEPS + n + 1)
                dve.tensor_tensor(picked[:, s % 2, :, :, :],
                                  sel[0:POS, 2 * (s % 2):2 * (s % 2) + 2, 0:4 * U].rearrange("p q (c u) -> p q c u", c=4),
                                  onehot_lo[:, n % 4, q0:q0 + 2, :, :, :].rearrange("p q j v c -> p q c (j v)"),
                                  ALU.mult).then_inc(picked_ready, 1)
                dve.wait_ge(picked_ready, k + 1)
                dve.tensor_reduce(score[:, n % 2, q0:q0 + 2, :].rearrange("p q c -> p (q c)"),
                                  picked[:, s % 2, :, :, :].rearrange("p q c u -> p (q c) u"), AX.X, ALU.add
                                  ).then_inc(score_ready, 1)

            def scale(t, n):
                k = t * STEPS + n
                dve.wait_ge(parts_ready, k + 1)
                if not (isinstance(k, int) and k < 2):
                    dve.wait_ge(wsum_full, 2 * k - 2)
                for q in range(4):
                    ins = dve.tensor_tensor(
                        scaled_lo[:, n % 2, q, :, :, :],
                        onehot_lo[:, n % 4, q, :, :, :].rearrange("p j v c -> p (j v) c").unsqueeze(1)
                        .to_broadcast([POS, 3, U, 4]),
                        parts[:, n % 2, q, :, :].unsqueeze(2).to_broadcast([POS, 3, U, 4]), ALU.mult)
                ins.then_inc(scaled_ready, 1)

            def step(t, n, last=False):
                pick(t, 2 * n)
                pick(t, 2 * n + 1)
                if n < STEPS - 2:
                    onehots(t, n + 2)
                elif not last:
                    onehots(t + 1, n + 2 - STEPS)
                scale(t, n)

            dve.memset(w2col[:, :], 0.0).then_inc(dve_tail_pre, 1)
            dve.memset(wd[:, :], 0.0).then_inc(dve_tail_pre, 1)
            dve.wait_ge(dve_tail_pre, 2)
            dve.memset(w2col[:, E:E + 1], 1.0).then_inc(attw_ready, 1)
            dve.memset(table_blk[:, :, :, :], 0.0).then_inc(blk_zero, 1)
            dve.memset(hiT[:, :, 8 * POS:], 0.0).then_inc(dve_tail_pre, 1)
            dve.memset(onehot_hi[:, :, 4 * HJ * 4:], 0.0).then_inc(dve_tail_pre, 1)
            dve.memset(tableT[E:E + 1, :, :], 0.0).then_inc(dve_tail_pre, 1)
            dve.memset(item_now[E:E + 1, :], 1.0)
            dve.wait_ge(dve_tail_pre, 5)
            dve.memset(tableT[E:E + 1, :, (NF - 1) * HI:NF * HI], 1.0).then_inc(blk_zero, 1)
            dve.wait_ge(weights_in, (NF + 3) * 16)
            flat = [wa[:, a, :, :].rearrange("p j e -> p (j e)") for a in range(4)]
            dve.tensor_tensor(wd[0:HID, 0:E], flat[1], flat[2], ALU.subtract).then_inc(attw_ready, 1)
            dve.tensor_tensor(flat[0], flat[0], flat[2], ALU.add).then_inc(attw_ready, 1)
            dve.wait_ge(vcol_ready, 1)
            dve.wait_ge(const_ready, 1)
            dve.tensor_scalar(mapq[0:E, 0:E], identf[0:E, 0:E], vcol[:, 1:2], None, ALU.mult).then_inc(mapq_ready, 1)
            for hb in range(2):
                dve.memset(scoretab[:, hb, :, :, :, :].rearrange("p q k u b -> p (q k u b)").bitcast(F32), 0.0
                           ).then_inc(scoretab_zero, 1)
            dve.wait_ge(const_ready, 2)

            onehots(0, 0)
            onehots(0, 1)
            for n in range(2):
                step(0, n)
            with dve.Fori(0, TILES - 1) as t:
                for n in range(2, STEPS + 2):
                    step(t + n // STEPS, n % STEPS)
            for n in range(2, STEPS):
                step(TILES - 1, n, last=True)

            tail_n = [5]

            def chain(ins):
                tail_n[0] += 1
                ins.then_inc(dve_tail_pre, 1)
                dve.wait_ge(dve_tail_pre, tail_n[0])

            def moments(x, rows, m0, m1, stage):
                for m in range(m0, m1):
                    for q in range(4):
                        ins = dve.bn_stats(stats[0:rows, m, q, :], x(m)[:, q * 512:(q + 1) * 512])
                chain(ins)
                for m in range(m0, m1):
                    ins = dve.bn_aggr(mv[0:rows, m, :], stats[0:rows, m, :, :].rearrange("p q s -> p (q s)"))
                chain(ins)
                dve.tensor_scalar(dice[0:rows, m0:m1, 0], mv[0:rows, m0:m1, 1], float(B) / (B - 1), EPS,
                                  ALU.mult, ALU.add).then_inc(dve_tail, 1)

            def affine(rows, m0, m1, gamma, beta, alpha):
                d = dice[0:rows, m0:m1, :]
                dve.tensor_scalar(d[:, :, 5], alpha, -1.0, 1.0, ALU.mult, ALU.add)
                chain(dve.reciprocal(d[:, :, 2], d[:, :, 1]))
                chain(dve.tensor_tensor(d[:, :, 3], d[:, :, 2], gamma, ALU.mult))
                chain(dve.tensor_tensor(d[:, :, 6], mv[0:rows, m0:m1, 0], d[:, :, 3], ALU.mult))
                dve.tensor_tensor(d[:, :, 4], beta, d[:, :, 6], ALU.subtract).then_inc(dve_tail, 1)

            dve.wait_ge(misc_copied, misc_before(TILES - 1, 8) + 1 + len(FIN))
            moments(lambda m: x1[:, m, :], MH, 0, 2, 0)
            dve.wait_ge(root_ready, 1)
            affine(MH, 0, 2, par1[:, 2, :], par1[:, 3, :], par1[:, 1, :])
            for q in range(4):
                for m in range(2):
                    c = slice(q * 512, (q + 1) * 512)
                    dve.wait_ge(gate_ready, 2 * q + m + 1)
                    chain(dve.tensor_scalar(gate1[:, m, c], gate1[:, m, c], dice[0:MH, m, 5:6], par1[:, 1, m:m + 1],
                                            ALU.mult, ALU.add))
                    dve.tensor_tensor(norm1[:, m, c], norm1[:, m, c], gate1[:, m, c], ALU.mult).then_inc(y_ready, 1)
            dve.wait_ge(head_copied, 4)
            moments(lambda m: x2, H2, 2, 3, 1)
            dve.wait_ge(root_ready, 2)
            affine(H2, 2, 3, par2[:, 2:3], par2[:, 3:4], par2[:, 1:2])
            for q in range(4):
                c = slice(q * 512, (q + 1) * 512)
                dve.wait_ge(gate_ready, 8 + q + 1)
                chain(dve.tensor_scalar(gate2[:, c], gate2[:, c], dice[0:H2, 2, 5:6], par2[:, 1:2], ALU.mult, ALU.add))
                dve.tensor_tensor(norm2[:, c], norm2[:, c], gate2[:, c], ALU.mult).then_inc(y_ready, 1)


_INS = ['r_user', 'r_item', 'r_rec_his', 'L0_rec_table_user', 'L0_rec_table_i1', 'L0_rec_table_i2',
        'L0_rec_table_i3', 'L0_rec_w_att1', 'L0_rec_b_att1', 'L0_rec_w_att2', 'L0_rec_b_att2', 'L0_rec_w1',
        'L0_rec_b1', 'L0_rec_a1', 'L0_rec_g1', 'L0_rec_be1', 'L0_rec_w2', 'L0_rec_b2', 'L0_rec_a2',
        'L0_rec_g2', 'L0_rec_be2', 'L0_rec_w3', 'L0_rec_b3']


def kernel(**inputs):
    import numpy as np
    import concourse.bacc as bacc
    from concourse.bass_utils import run_bass_kernel_spmd

    nc = bacc.Bacc("TRN2", target_bir_lowering=False, num_devices=1)
    arrays, args = {}, []
    for name in _INS:
        a = np.ascontiguousarray(inputs[name])
        arrays[f"in_{name}_dram"] = a
        args.append(nc.dram_tensor(f"in_{name}_dram", a.shape, mybir.dt.from_np(a.dtype), kind="ExternalInput").ap())
    rows = inputs["r_user"].shape[0]
    out = nc.dram_tensor("out_0_dram", (rows,), F32, kind="ExternalOutput").ap()
    build(nc, *args, out)
    r = run_bass_kernel_spmd(nc, [arrays], core_ids=[0])
    return r.results[0]["out_0_dram"]
```

```python
from contextlib import ExitStack

import concourse.bass as bass
from concourse import mybir

F32 = mybir.dt.float32
BF16 = mybir.dt.bfloat16
I32 = mybir.dt.int32
U32 = mybir.dt.uint32
ALU = mybir.AluOpType
ACT = mybir.ActivationFunctionType
AX = mybir.AxisListType

FEAT = (1, 2, 0)


def build(nc, r_user, r_item, r_his, table_user, table_i1, table_i2, table_i3, w_att1, b_att1,
          w_att2, b_att2, w1, b1, a1, g1, be1, w2, b2, a2, g2, be2, w3, b3, out):
    B, HIST, NF = r_his.shape
    V, D = table_i1.shape
    VU, DU = table_user.shape
    HID = w_att1.shape[0]
    H1, H2 = w1.shape[0], w2.shape[0]
    tables = (table_i1, table_i2, table_i3)
    E = NF * D
    EPS = 1e-8
    ROUND = 1.5 * 2.0 ** 23

    POS = HIST // 2
    HI, LO = 40, 25
    MID = LO // 2
    FAR = 2.0 ** 100
    HB = HI + 2
    HJ, U = NF * HB, NF * LO
    TILE, HALF = 128, 64
    TILES = B // TILE
    STEPS = 16
    SLOTS = 32
    QUADS = HALF // 2
    MH = H1 // 2
    ROUNDS = ((0, 7), (7, 13), (13, 19), (19, 25))
    assert HI * LO == V and HJ <= 126 and STEPS * 8 == TILE and 2 * POS == HIST

    with ExitStack() as ctx:
        def sb(name, shape, dt=F32):
            return ctx.enter_context(nc.sbuf_tensor(name, shape, dt))

        def pb(name, shape, dt=F32):
            return ctx.enter_context(nc.psum_tensor(name, shape, dt))

        def sem(name):
            return ctx.enter_context(nc.semaphore(name))

        scoretab = sb("scoretab", [128, 2, HALF // 4, 3, U, 4], BF16)
        scores_f = sb("scores_f", [HJ, HALF // 4, LO, 4])
        scores_b = sb("scores_b", [HJ, HALF // 4, 3, LO, 4], BF16)
        wsum_ring = sb("wsum_ring", [128, 2, U, TILE // 4])
        weightsum = sb("weightsum", [128, 4, LO, TILE // 4])
        onehot_hi = sb("onehot_hi", [POS, 4, 4 * HJ * 4 + 8], BF16)
        onehot_lo = sb("onehot_lo", [POS, 2, 4, NF, LO, 4], BF16)
        scaled_lo = sb("scaled_lo", [POS, 2, 4, 3, U, 4], BF16)
        hiT = sb("hiT", [128, 2, 8 * POS + 128 - POS], BF16)
        score_j = sb("score_j", [POS, 2, 4, 4, NF])
        score_2 = sb("score_2", [POS, 4, 4])
        score = sb("score", [POS, 4, 4])
        score_m = sb("score_m", [POS, 4, 4])
        score_r = sb("score_r", [POS, 4, 4])
        parts = sb("parts", [POS, 2, 4, 3, 4], BF16)
        digits = sb("digits", [POS, 2, 2, QUADS, NF, 4], BF16)
        lo_terms = sb("lo_terms", [POS, 2, QUADS, NF, 2, 4], BF16)
        far_rows = sb("far_rows", [HI, 3, LO], BF16)
        far = sb("far", [128, U], BF16)
        keep = sb("keep", [POS, 2, QUADS, 4])
        raw = sb("raw", [HALF, HIST * NF], I32)
        raw_f = sb("raw_f", [HALF, HIST * NF])
        digit_f = raw[:, :].bitcast(F32)
        digits_b = sb("digits_b", [HALF, 2, HIST * NF], BF16)
        iota_i = sb("iota_i", [POS, HI, 4], I32)
        iota_hi = sb("iota_hi", [POS, HI, 4], BF16)
        iota_lo = sb("iota_lo", [POS, LO, 4], BF16)
        identf = sb("identf", [128, 128])
        identb = sb("identb", [128, 128], BF16)
        table_blk = sb("table_blk", [HJ, LO, NF, D])
        tableT = sb("tableT", [E + 1, LO, HJ])
        item_ids = sb("item_ids", [TILE, TILES, NF], I32)
        user_ids = sb("user_ids", [TILE, TILES], I32)
        ids_f = sb("ids_f", [TILE, TILES])
        ids_raw = sb("ids_raw", [TILE, TILES])
        ids_neg = sb("ids_neg", [TILE, TILES])
        ids_u = sb("ids_u", [TILE, TILES, NF + 1], U32)
        ids_now = sb("ids_now", [TILE, NF + 1], U32)
        item_rows = sb("item_rows", [TILE, NF, D])
        user_rows = sb("user_rows", [TILE, DU])
        item_now = sb("item_now", [E + 1, TILE])
        item_last = sb("item_last", [E, TILE])
        queryT = sb("queryT", [E + 1, TILE])
        mapq = sb("mapq", [E + 1, E + 1])
        vcol = sb("vcol", [E, 2])
        wa = sb("wa", [HID, 4, NF, D])
        wd = sb("wd", [HID + 1, E + 1])
        w2col = sb("w2col", [HID + 1, E + 1])
        browseT = sb("browseT", [E, TILE])
        userT = sb("userT", [DU, TILE])
        weights_flat = weightsum[:, :, :, :].rearrange("p w l b -> p (w l b)")
        w1_rows = weights_flat[0:MH, 0:2 * (2 * E + DU)].rearrange("p (m k) -> p m k", m=2)
        w1T = sb("w1T", [E, 3, 2, MH])
        w2_rows = weights_flat[0:H2, 1024:1024 + H1]
        w2T = sb("w2T", [MH, 2, H2])
        w3T = sb("w3T", [H2, 1])
        par1 = sb("par1", [MH, 4, 2])
        par2 = sb("par2", [H2, 4])
        b3s = sb("b3s", [1, 1])
        x1 = sb("x1", [MH, 2, B])
        stats = sb("stats", [128, 3, 4, 6])
        mv = sb("mv", [128, 3, 2])
        dice = sb("dice", [128, 3, 8])
        probs = table_blk[0:1, :, :, :].rearrange("p l j e -> p (l j e)")[:, 0:B]
        tail1 = scoretab[0:MH, :, :, :, :, :].rearrange("p a b c d e -> p (a b c d e)").bitcast(F32)
        gate1 = tail1[:, 0:2 * B].rearrange("p (m b) -> p m b", m=2)
        norm1 = tail1[:, 2 * B:4 * B].rearrange("p (m b) -> p m b", m=2)
        tail2 = wsum_ring[0:H2, :, :, :].rearrange("p a u b -> p (a u b)")
        x2, gate2 = tail2[:, 0:B], tail2[:, B:2 * B]
        norm2 = weightsum[0:H2, :, :, :].rearrange("p a l b -> p (a l b)")[:, 0:B]

        sel = pb("sel", [128, 4, 512])
        hiT_ps = pb("hiT_ps", [128, 2, 1024], BF16)
        wsum_ps = pb("wsum_ps", [128, 512])
        misc = pb("misc", [128, 512])

        weights_in = sem("weights_in")
        tables_in = sem("tables_in")
        small_in = sem("small_in")
        item_ids_in = sem("item_ids_in")
        user_ids_in = sem("user_ids_in")
        raw_in = sem("raw_in")
        item_rows_in = sem("item_rows_in")
        user_rows_in = sem("user_rows_in")
        blk_zero = sem("blk_zero")
        const_ready = sem("const_ready")
        pool_step = sem("pool_step")
        attw_ready = sem("attw_ready")
        vcol_ready = sem("vcol_ready")
        mapq_ready = sem("mapq_ready")
        ids_ready = sem("ids_ready")
        raw_f_ready = sem("raw_f_ready")
        digit_step = sem("digit_step")
        digits_b_ready = sem("digits_b_ready")
        keep_ready = sem("keep_ready")
        hi_ready = sem("hi_ready")
        lo_ready = sem("lo_ready")
        hiT_full = sem("hiT_full")
        hiT_copied = sem("hiT_copied")
        sel_full = sem("sel_full")
        lo_rows_ready = sem("lo_rows_ready")
        far_made = sem("far_made")
        far_in = sem("far_in")
        far_zero = sem("far_zero")
        score_ready = sem("score_ready")
        split_step = sem("split_step")
        parts_ready = sem("parts_ready")
        scaled_ready = sem("scaled_ready")
        wsum_full = sem("wsum_full")
        wsum_copied = sem("wsum_copied")
        scoretab_zero = sem("scoretab_zero")
        scores_split = sem("scores_split")
        scores_step = sem("scores_step")
        scoretab_in = sem("scoretab_in")
        weightsum_in = sem("weightsum_in")
        misc_full = sem("misc_full")
        misc_copied = sem("misc_copied")
        dve_tail = sem("dve_tail")
        dve_tail_pre = sem("dve_tail_pre")
        root_ready = sem("root_ready")
        y_ready = sem("y_ready")
        gate_ready = sem("gate_ready")
        head_full = sem("head_full")
        head_copied = sem("head_copied")
        pool_passed = sem("pool_passed")
        pe_passed = sem("pe_passed")
        sp_passed = sem("sp_passed")
        item_kept = sem("item_kept")
        out_done = sem("out_done")

        def hi_rows(s4):
            return onehot_hi[:, s4, 0:4 * HJ * 4].rearrange("p (g v c) -> p g v c", v=HB, c=4)

        prologue = (["attw"] + [("tableT", i) for i in range(7)] + [("digit", 0, 0), ("digit", 1, 0), "item", "query"]
                    + [("scoretab", r, 0) for r in range(4)] + ["w1T", "w1uT", "w2T"])
        DIGITS0 = prologue.index(("digit", 1, 0)) + 1
        ITEM0 = prologue.index("item") + 1
        QUERY0 = prologue.index("query") + 1

        def bank(seq):
            b = sel[:, seq % 4, :] if isinstance(seq, int) and seq < len(prologue) else misc[:, :]
            return b, b.bitcast(BF16)

        FIN = ["finish", "layer1"]
        OWN = 30
        in_slot = {1: ("scoretab", 0, 1), 3: ("scoretab", 1, 1), 5: ("scoretab", 2, 1), 7: ("scoretab", 3, 1),
                   8: ("digit", 0, 1), 9: ("digit", 1, 1), 14: "finish", 15: "layer1",
                   16: "item", 17: "query", 19: ("scoretab", 0, 0), 21: ("scoretab", 1, 0),
                   22: ("digit", 0, 0), 23: ("digit", 1, 0), 25: ("scoretab", 2, 0), 27: ("scoretab", 3, 0),
                   OWN: "userT"}
        span = {}
        for end, what in in_slot.items():
            parts_n = {"f": 5, "s": 2}.get(what[0][0], 1)
            for i in range(parts_n):
                span[end - parts_n + 1 + i] = (end, i, parts_n)
        order = sorted(in_slot)
        PER_TILE = len(order)

        def misc_before(t, slot):
            return t * PER_TILE + (len(prologue) + order.index(slot))

        N_SMALL = 2 * NF + 1 + 3 + 8
        FIRST = 16
        EARLY = 3
        SC_LAG = 3

        ctx.enter_context(nc.allow_non_contiguous_dma(reason="a few hundred weights and ids, loaded once"))
        block = ctx.enter_context(nc.Block())

        @block.sync
        def _(sp):
            def await_ge(signal, value):
                sp.wait_ge(signal, value)
                if not isinstance(value, int):
                    sp.sem_inc(sp_passed, 1)

            his_rows = r_his.rearrange("b l f -> b (l f)")
            sp.dma_start(raw[:, :], his_rows[0:HALF, :]).then_inc(raw_in, 16)
            sp.dma_start(item_ids[:, :, :], r_item.rearrange("(t p) f -> p t f", p=TILE)).then_inc(item_ids_in, 16)
            wsrc = w_att1.rearrange("h (a f e) -> h a f e", a=4, f=NF)
            for j in range(NF):
                sp.dma_start(wa[:, :, j, :], wsrc[:, :, FEAT[j], :]).then_inc(weights_in, 16)
            sp.wait_ge(attw_ready, 1)
            sp.dma_start(w2col[0:HID, E:E + 1], w_att2.rearrange("o h -> h o")).then_inc(weights_in, 16)
            sp.dma_start(wd[0:HID, E:E + 1], b_att1.rearrange("(h o) -> h o", o=1)).then_inc(weights_in, 16)
            sp.dma_start(wd[HID:HID + 1, E:E + 1], b_att2.rearrange("(h o) -> h o", o=1)).then_inc(weights_in, 16)
            sp.wait_ge(blk_zero, 1)
            for j in range(NF):
                src = tables[FEAT[j]]
                sp.dma_start(table_blk[j * HB:j * HB + HI, :, j, :],
                             src.rearrange("(h l) e -> h l e", l=LO)).then_inc(tables_in, 16)
            sp.wait_ge(far_made, 3)
            for j in range(NF):
                c = slice(j * LO, (j + 1) * LO)
                sp.dma_start(far[j * HB:j * HB + HI, c], far_rows[:, 0, :]).then_inc(far_in, 16)
                sp.dma_start(far[j * HB + HI:(j + 1) * HB, c], far_rows[0:1, 1:3, :]).then_inc(far_in, 16)

            def load_rows(h):
                await_ge(digits_b_ready, 2 * h)
                sp.dma_start(raw[:, :], his_rows[bass.ds(h * HALF, HALF), :]).then_inc(raw_in, 16)

            def place_scores(t, hb):
                g = 2 * t + hb
                await_ge(scores_split, 4 * g + 4)
                if isinstance(g, int) and g < 2:
                    sp.wait_ge(scoretab_zero, hb + 1)
                else:
                    await_ge(sel_full, 16 * g - 16)
                for j in range(NF):
                    r = slice(j * HB, j * HB + HI)
                    sp.dma_start(scoretab[r, hb, :, :, j * LO:(j + 1) * LO, :].rearrange("p q k l b -> p (q k) (l b)"),
                                 scores_b[r, :, :, :, :].rearrange("p q k l b -> p (q k) (l b)")
                                 ).then_inc(scoretab_in, 16)

            def collect_sums(t, w):
                k = 4 * t + w
                await_ge(wsum_copied, 8 * k + 8)
                if not (isinstance(k, int) and k < 1):
                    await_ge(weightsum_in, NF * 16 * k)
                if w == 0 and not (isinstance(t, int) and t == 0):
                    await_ge(misc_full, misc_before(t, 14) + 1)
                for j in range(NF):
                    r = slice(j * HB, (j + 1) * HB)
                    sp.dma_start(weightsum[r, w, :, :].rearrange("p l b -> p (l b)"),
                                 wsum_ring[r, w % 2, j * LO:(j + 1) * LO, :].rearrange("p l b -> p (l b)")
                                 ).then_inc(weightsum_in, 16)

            def tile(t, last=False):
                if not last:
                    load_rows(2 * t + 2)
                if not (isinstance(t, int) and t == 0):
                    collect_sums(t - 1, 3)
                place_scores(t, 1)
                collect_sums(t, 0)
                collect_sums(t, 1)
                if not last:
                    load_rows(2 * t + 3)
                collect_sums(t, 2)
                if not last:
                    place_scores(t + 1, 0)

            load_rows(1)
            place_scores(0, 0)
            tile(0)
            with sp.Fori(1, TILES - 1) as t:
                tile(t)
            tile(TILES - 1, last=True)
            collect_sums(TILES - 1, 3)
            sp.wait_ge(head_copied, 8)
            sp.dma_start(out.rearrange("(o b) -> o b", o=1), probs).then_inc(out_done, 16)
            sp.wait_ge(out_done, 16)

        @block.gpsimd
        def _(pool):
            n_step = [0]

            def await_ge(signal, value):
                pool.wait_ge(signal, value)
                if not isinstance(value, int):
                    pool.sem_inc(pool_passed, 1)

            def chain(ins):
                n_step[0] += 1
                ins.then_inc(pool_step, 1)
                pool.wait_ge(pool_step, n_step[0])

            def make_digits(h, first, end):
                for op in range(first, end):
                    if op == 0:
                        await_ge(raw_in, (h + 1) * 16)
                        pool.tensor_scalar(raw_f[:, :], raw[:, :], -float(MID), None, ALU.add).then_inc(raw_f_ready, 1)
                    elif op == 1:
                        await_ge(raw_f_ready, h + 1)
                        pool.tensor_scalar(digit_f, raw_f[:, :], 1.0 / LO, ROUND, ALU.mult, ALU.add
                                           ).then_inc(digit_step, 1)
                    elif op == 2:
                        await_ge(digit_step, 2 * h + 1)
                        pool.tensor_scalar(digits_b[:, 1, :], digit_f, -ROUND, None, ALU.add
                                           ).then_inc(digits_b_ready, 1)
                    elif op == 3:
                        await_ge(digits_b_ready, 2 * h + 1)
                        pool.tensor_scalar(digit_f, digit_f, -ROUND, float(LO), ALU.add, ALU.mult
                                           ).then_inc(digit_step, 1)
                    else:
                        await_ge(digit_step, 2 * h + 2)
                        pool.tensor_tensor(digits_b[:, 0, :], raw_f[:, :], digit_f, ALU.subtract
                                           ).then_inc(digits_b_ready, 1)

            def make_keep(n, hb):
                d = [digits[:, hb, k, :, NF - 1, :] for k in range(2)]
                pool.tensor_tensor(keep[:, hb, :, :], d[0], d[1], ALU.add).then_inc(keep_ready, 1)
                await_ge(keep_ready, 2 * n + 1)
                pool.tensor_scalar(keep[:, hb, :, :], keep[:, hb, :, :], -float(MID), None, ALU.is_gt
                                   ).then_inc(keep_ready, 1)

            def gather_items(t, features):
                if features[0] == 0:
                    pool.tensor_copy(ids_now[:, 0:NF], ids_u[:, bass.ds(t, 1), 0:NF].rearrange("p o f -> p (o f)")
                                     ).then_inc(ids_ready, 1)
                    await_ge(ids_ready, 1 if isinstance(t, int) and t == 0 else 2 * t)
                for j in features:
                    pool.indirect_dma_start(out=item_rows[:, j, :], out_offset=None, in_=tables[FEAT[j]],
                                            in_offset=bass.IndirectOffsetOnAxis(ap=ids_now[:, j:j + 1], axis=0)
                                            ).then_inc(item_rows_in, 16)

            def gather_users(t):
                pool.tensor_copy(ids_now[:, NF:NF + 1], ids_u[:, bass.ds(t, 1), NF:NF + 1].rearrange("p o f -> p (o f)")
                                 ).then_inc(ids_ready, 1)
                await_ge(ids_ready, 2 * TILES if isinstance(t, int) else 2 * t + 3)
                pool.indirect_dma_start(out=user_rows[:, :], out_offset=None, in_=table_user,
                                        in_offset=bass.IndirectOffsetOnAxis(ap=ids_now[:, NF:NF + 1], axis=0)
                                        ).then_inc(user_rows_in, 16)

            def split(t, n):
                k = t * STEPS + n
                hb, q0, p2 = n // 8, (n % 8) * 4, n % 2
                if n in (0, 8):
                    await_ge(keep_ready, (2 * t + hb + 1) * 2)
                pool.wait_ge(score_ready, 2 * k + 2)
                if not (isinstance(k, int) and k < 2):
                    pool.wait_ge(scaled_ready, k - 1)
                kp = keep[:, hb, q0:q0 + 4, :]
                pool.tensor_tensor(score_2[:, :, :], score_j[:, p2, :, :, 0], score_j[:, p2, :, :, 1], ALU.add
                                   ).then_inc(split_step, 1)
                pool.wait_ge(split_step, 4 * k + 1)
                pool.tensor_tensor(score[:, :, :], score_2[:, :, :], score_j[:, p2, :, :, 2], ALU.add
                                   ).then_inc(split_step, 1)
                pool.wait_ge(split_step, 4 * k + 2)
                pool.tensor_tensor(score_m[:, :, :], score[:, :, :], kp, ALU.mult)
                pool.tensor_tensor(parts[:, p2, :, 0, :], score[:, :, :], kp, ALU.mult).then_inc(split_step, 1)
                pool.wait_ge(split_step, 4 * k + 3)
                pool.tensor_tensor(score_r[:, :, :], score_m[:, :, :], parts[:, p2, :, 0, :], ALU.subtract)
                pool.tensor_tensor(parts[:, p2, :, 1, :], score_m[:, :, :], parts[:, p2, :, 0, :], ALU.subtract
                                   ).then_inc(split_step, 1)
                pool.wait_ge(split_step, 4 * k + 4)
                pool.tensor_tensor(parts[:, p2, :, 2, :], score_r[:, :, :], parts[:, p2, :, 1, :], ALU.subtract
                                   ).then_inc(parts_ready, 1)

            def split_scores(copied, g, r):
                k = 4 * g + r
                lo = slice(*ROUNDS[r])
                full, part = scores_f[:, :, lo, :], [scores_b[:, :, i, lo, :] for i in range(3)]
                await_ge(misc_copied, copied)
                pool.tensor_tensor(part[1], full, part[0], ALU.subtract).then_inc(scores_step, 1)
                await_ge(scores_step, 2 * k + 1)
                pool.tensor_tensor(full, full, part[0], ALU.subtract).then_inc(scores_step, 1)
                await_ge(scores_step, 2 * k + 2)
                pool.tensor_tensor(part[2], full, part[1], ALU.subtract).then_inc(scores_split, 1)

            def step(t, n, last=False):
                split(t, n)
                if n in (1, 2, 3, 4):
                    split_scores(misc_before(t, 2 * n - 1) + 1, 2 * t + 1, n - 1)
                if n in (10, 11, 12, 13) and not last:
                    split_scores(misc_before(t, (19, 21, 25, 27)[n - 10]) + 1, 2 * t + 2, n - 10)
                if n == 0:
                    make_digits(2 * t + 1, 4, 5)
                if n == 3 and not last:
                    await_ge(misc_full, item_read(t))
                    gather_items(t + 1, (0,))
                if n == 5 and not last:
                    gather_items(t + 1, (1, 2))
                    make_digits(2 * t + 2, 0, 1)
                if n == 6:
                    if not (isinstance(t, int) and t == 0):
                        await_ge(misc_full, misc_before(t - 1, OWN) + 1)
                    gather_users(t)
                if n == 7:
                    await_ge(misc_copied, misc_before(t, 9) + 1)
                    make_keep(2 * t + 1, 1)
                if n in (6, 7, 8, 9) and not last:
                    if n == 7:
                        await_ge(misc_full, misc_before(t, 9) + 1)
                    make_digits(2 * t + 2, n - 5, n - 4)
                if n == 14 and not last:
                    await_ge(misc_copied, misc_before(t, 23) + 1)
                    make_keep(2 * t + 2, 0)
                    make_digits(2 * t + 3, 0, 2)
                if n == 15 and not last:
                    await_ge(misc_full, misc_before(t, 23) + 1)
                    make_digits(2 * t + 3, 2, 4)

            def item_read(t):
                return ITEM0 if isinstance(t, int) and t == 0 else misc_before(t - 1, 16) + 1

            chain(pool.memset(identf[:, :], 0.0))
            chain(pool.affine_select(out=identf[:, :], in_=identf[:, :], compare_op=ALU.not_equal, fill=1.0,
                                     base=0, pattern=[[-1, 128]], channel_multiplier=1))
            pool.tensor_copy(identb[:, :], identf[:, :]).then_inc(const_ready, 1)
            chain(pool.iota(iota_i[:, :, :], pattern=[[1, HI], [0, 4]], base=0, channel_multiplier=0))
            chain(pool.tensor_copy(iota_hi[:, :, :], iota_i[:, :, :]))
            chain(pool.iota(iota_i[:, 0:LO, :], pattern=[[1, LO], [0, 4]], base=-MID, channel_multiplier=0))
            chain(pool.tensor_copy(iota_lo[:, :, :], iota_i[:, 0:LO, :]))
            column = iota_lo[0:HI, :, 0]
            chain(pool.tensor_tensor(far_rows[:, 0, :], column, column, ALU.mult))
            pool.tensor_scalar(far_rows[:, 0, :], far_rows[:, 0, :], -FAR, None, ALU.mult).then_inc(far_made, 1)
            pool.tensor_scalar(far_rows[:, 1, :], column, 2.0 * FAR, None, ALU.mult).then_inc(far_made, 1)
            pool.sem_inc(const_ready, 1)
            make_digits(0, 0, 5)
            await_ge(item_ids_in, 16)
            for c in range(NF + 1):
                rows = V if c < NF else VU
                src = item_ids[:, :, FEAT[c]] if c < NF else user_ids[:, :]
                if c == NF:
                    gather_items(0, (0, 1, 2))
                    await_ge(user_ids_in, 16)
                chain(pool.tensor_copy(ids_raw[:, :], src))
                chain(pool.tensor_scalar(ids_neg[:, :], ids_raw[:, :], 0.0, float(rows), ALU.is_lt, ALU.mult))
                chain(pool.tensor_tensor(ids_f[:, :], ids_raw[:, :], ids_neg[:, :], ALU.add))
                chain(pool.tensor_scalar(ids_u[:, :, c], ids_f[:, :], 0.0, float(rows - 1), ALU.max, ALU.min))
            await_ge(misc_copied, DIGITS0)
            make_keep(0, 0)
            for r in range(4):
                split_scores(QUERY0 + 1 + r, 0, r)
            make_digits(1, 0, 4)
            for n in range(2):
                step(0, n)
            with pool.Fori(0, TILES - 1) as t:
                for n in range(2, STEPS + 2):
                    step(t + n // STEPS, n % STEPS)
            for n in range(2, STEPS):
                step(TILES - 1, n, last=True)

        @block.tensor
        def _(pe):
            def await_ge(signal, value):
                pe.wait_ge(signal, value)
                if not isinstance(value, int):
                    pe.sem_inc(pe_passed, 1)

            def hi_columns(s4, q, c):
                return onehot_hi[:, s4, q * HJ * 4 + c:q * HJ * 4 + c + 127 * 4 + 1:4]

            def transpose_hi(t, s):
                k = t * SLOTS + s
                pe.wait_ge(hi_ready, t * STEPS + s // 2 + 1)
                pe.wait_ge(lo_rows_ready, t * STEPS + s // 2 + 1)
                if not (isinstance(k, int) and k < 2):
                    pe.wait_ge(hiT_copied, k - 1)
                for c in range(8):
                    q = (s % 2) * 2 + c // 4
                    mm = pe.transpose(hiT_ps[:, s % 2, c * POS:(c + 1) * POS], hi_columns((s // 2) % 4, q, c % 4),
                                      identb[0:POS, 0:POS])
                mm.then_inc(hiT_full, 1)

            def read_scores(t, s):
                k = t * SLOTS + s
                pe.wait_ge(hiT_copied, k + 1)
                if s in (0, 16):
                    pe.wait_ge(scoretab_in, (2 * t + s // 16 + 1) * (NF * 16))
                if not (isinstance(k, int) and k < 2):
                    pe.wait_ge(score_ready, k - 1)
                for c in range(8):
                    b = (s % 16) * 4 + c // 2
                    o = sel[:, 2 * (s % 2) + c // 4, (c % 4) * U:(c % 4 + 1) * U]
                    rows = hiT[0:HJ, s % 2, c * POS:c * POS + 128]
                    pe.matmul(o, rows, far[0:HJ, :], start=True, stop=False)
                    for i in range(3):
                        mm = pe.matmul(o, rows, scoretab[0:HJ, s // 16, b // 4, i, :, b % 4],
                                       start=False, stop=(i == 2))
                mm.then_inc(sel_full, 1)

            def add_scores(t, s):
                k = t * SLOTS + s
                n = s // 2
                pe.wait_ge(scaled_ready, t * STEPS + n + 1)
                if not (isinstance(k, int) and k < 1):
                    pe.wait_ge(wsum_copied, k)
                for b in range(4):
                    q = (s % 2) * 2 + b // 2
                    for i in range(6):
                        c = (b % 2) * 2 + i // 3
                        mm = pe.matmul(wsum_ps[:, b * U:(b + 1) * U], hi_columns(n % 4, q, c),
                                       scaled_lo[:, n % 2, q, i % 3, :, c], start=(i == 0), stop=(i == 5))
                mm.then_inc(wsum_full, 1)

            def task(what, seq, t, part=0, parts_n=1):
                def share(items):
                    return items[part * len(items) // parts_n:(part + 1) * len(items) // parts_n]

                misc, misc_b = bank(seq)
                name = what if isinstance(what, str) else what[0]
                if isinstance(seq, int) and seq < len(prologue):
                    copied = {"query": ITEM0, "scoretab": QUERY0}.get(name, 0)
                    if max(copied, seq - 3) > 0:
                        await_ge(misc_copied, max(copied, seq - 3))
                elif part == 0:
                    await_ge(misc_copied, seq)
                if name == "attw":
                    await_ge(attw_ready, 3)
                    pe.matmul(misc[0:E, 0:1], wa[:, 0, :, :].rearrange("p j e -> p (j e)"), w2col[0:HID, E:E + 1],
                              start=True, stop=True)
                    pe.matmul(misc[0:E, 1:2], wa[:, 3, :, :].rearrange("p j e -> p (j e)"), w2col[0:HID, E:E + 1],
                              start=True, stop=True)
                    mm = pe.matmul(misc[0:E + 1, 2:E + 3], w2col[:, :], wd[:, :], start=True, stop=True)
                elif name == "tableT":
                    await_ge(tables_in, NF * 16)
                    for i in range(min(4, LO - 4 * what[1])):
                        lo = what[1] * 4 + i
                        mm = pe.transpose(misc[0:E, i * HJ:(i + 1) * HJ],
                                          table_blk[:, lo, :, :].rearrange("p j e -> p (j e)"), identf[0:HJ, 0:HJ])
                elif name == "w1T":
                    await_ge(small_in, 16 * N_SMALL)
                    for m in range(2):
                        for g in range(2):
                            i = g * 2 + m
                            mm = pe.transpose(misc[0:E, i * MH:(i + 1) * MH], w1_rows[:, m, g * E:(g + 1) * E],
                                              identf[0:MH, 0:MH])
                elif name == "w1uT":
                    for m in range(2):
                        mm = pe.transpose(misc[0:DU, m * MH:(m + 1) * MH], w1_rows[:, m, 2 * E:2 * E + DU],
                                          identf[0:MH, 0:MH])
                elif name == "w2T":
                    for m in range(2):
                        mm = pe.transpose(misc[0:MH, m * H2:(m + 1) * H2], w2_rows[:, m * MH:(m + 1) * MH],
                                          identf[0:H2, 0:H2])
                elif name == "digit":
                    hb, kind = what[2], what[1]
                    await_ge(digits_b_ready, (t * 2 + hb) * 2 + 2)
                    src = digits_b[:, kind, :].rearrange("p (c l f) -> p f c l", c=2, f=NF)
                    for j in range(NF):
                        for c in range(2):
                            i = j * 2 + c
                            mm = pe.transpose(misc_b[0:POS, i * HALF:(i + 1) * HALF], src[:, FEAT[j], c, :],
                                              identb[0:HALF, 0:HALF])
                elif name == "item":
                    await_ge(item_rows_in, (t + 1) * (NF * 16))
                    mm = pe.transpose(misc[0:E, 0:TILE], item_rows[:, :, :].rearrange("p j e -> p (j e)"),
                                      identf[:, :])
                elif name == "query":
                    if isinstance(t, int) and t == 0:
                        await_ge(mapq_ready, 1)
                    mm = pe.matmul(misc[0:E + 1, 0:TILE], mapq[:, :], item_now[:, :], start=True, stop=True)
                elif name == "scoretab":
                    r, hb = what[1], what[2]
                    for i, lo in share(list(enumerate(range(*ROUNDS[r])))):
                        mm = pe.matmul(misc[0:HJ, i * HALF:(i + 1) * HALF], tableT[:, lo, :],
                                       queryT[:, hb * HALF:(hb + 1) * HALF], start=True, stop=True)
                elif name == "finish":
                    if part == 0:
                        await_ge(weightsum_in, (t + 1) * (4 * NF * 16))
                    for lo in share(range(LO)):
                        mm = pe.matmul(misc[0:E, 0:TILE].rearrange("p (w b) -> p w b", w=4),
                                       table_blk[:, lo, :, :].rearrange("p j e -> p (j e)"),
                                       weightsum[0:HJ, :, lo, :], start=(lo == 0), stop=(lo == LO - 1))
                elif name == "userT":
                    await_ge(user_rows_in, (t + 1) * 16)
                    mm = pe.transpose(misc[0:DU, 0:TILE], user_rows[:, :], identf[:, :])
                elif name == "layer1":
                    items = item_now[0:E, :] if isinstance(t, int) and t == TILES - 1 else item_last[:, :]
                    for m in range(2):
                        o = misc[0:MH, m * TILE:(m + 1) * TILE]
                        pe.matmul(o, w1T[:, 0, m, :], items, start=True, stop=False)
                        pe.matmul(o, w1T[:, 1, m, :], browseT[:, :], start=False, stop=False)
                        mm = pe.matmul(o, w1T[0:DU, 2, m, :], userT[:, :], start=False, stop=True)
                if part == parts_n - 1:
                    mm.then_inc(misc_full, 1)

            def slot(t, s, last=False):
                if s < SLOTS - 1:
                    transpose_hi(t, s + 1)
                elif not last:
                    transpose_hi(t + 1, 0)
                read_scores(t, s)
                if s in span:
                    end, part, parts_n = span[s]
                    what = in_slot[end]
                    if what in FIN:
                        if not (isinstance(t, int) and t == 0):
                            task(what, misc_before(t, end), t - 1, part, parts_n)
                        elif s == end:
                            pe.wait_ge(misc_full, misc_before(t, end))
                            pe.sem_inc(misc_full, 1)
                    elif s < 16:
                        task(what, misc_before(t, end), t, part, parts_n)
                    elif end == OWN:
                        task(what, misc_before(t, 16 if last else OWN), t)
                    elif not last:
                        task(what, misc_before(t, end), t + 1, part, parts_n)
                if s >= SC_LAG:
                    add_scores(t, s - SC_LAG)
                elif not (isinstance(t, int) and t == 0):
                    add_scores(t - 1, s - SC_LAG + SLOTS)

            pe.wait_ge(const_ready, 1)
            pe.wait_ge(far_in, 2 * NF * 16)
            for seq, what in enumerate(prologue):
                task(what, seq, 0)
            transpose_hi(0, 0)
            for s in range(FIRST):
                slot(0, s)
            with pe.Fori(0, TILES - 1) as t:
                for s in range(FIRST, SLOTS + FIRST):
                    slot(t + s // SLOTS, s % SLOTS)
            for s in range(FIRST, SLOTS):
                slot(TILES - 1, s, last=True)
            for s in range(SLOTS - SC_LAG, SLOTS):
                add_scores(TILES - 1, s)
            base = misc_before(TILES - 1, 16) + 1
            for i, what in enumerate(FIN):
                task(what, base + i, TILES - 1)
            for q in range(4):
                pe.wait_ge(y_ready, 2 * q + 2)
                for m in range(2):
                    mm = pe.matmul(sel[0:H2, q, :], w2T[:, m, :], norm1[:, m, q * 512:(q + 1) * 512],
                                   start=(m == 0), stop=(m == 1))
                mm.then_inc(head_full, 1)
            for q in range(4):
                pe.wait_ge(y_ready, 8 + q + 1)
                pe.wait_ge(head_copied, 4)
                pe.matmul(sel[0:1, q, :], w3T[:, :], norm2[:, q * 512:(q + 1) * 512],
                          start=True, stop=True).then_inc(head_full, 1)

        @block.scalar
        def _(act):
            act.dma_start(user_ids[:, :], r_user.rearrange("(t p) o -> p (t o)", p=TILE)).then_inc(user_ids_in, 16)
            n_small = 0
            for g in range(2):
                for j in range(NF):
                    act.dma_start(w1_rows[:, :, g * E + j * D:g * E + (j + 1) * D],
                                  w1.rearrange("(m p) k -> p m k", m=2)[:, :, g * E + FEAT[j] * D:g * E + (FEAT[j] + 1) * D]
                                  ).then_inc(small_in, 16)
                    n_small += 1
            act.dma_start(w1_rows[:, :, 2 * E:2 * E + DU], w1.rearrange("(m p) k -> p m k", m=2)[:, :, 2 * E:2 * E + DU]
                          ).then_inc(small_in, 16)
            act.dma_start(w2_rows, w2).then_inc(small_in, 16)
            act.dma_start(w3T[:, :], w3.rearrange("o h -> h o")).then_inc(small_in, 16)
            act.dma_start(b3s[:, :], b3.rearrange("(o h) -> o h", o=1)).then_inc(small_in, 16)
            n_small += 4
            for i, v in enumerate((b1, a1, g1, be1)):
                act.dma_start(par1[:, i, :], v.rearrange("(m p) -> p m", m=2)).then_inc(small_in, 16)
                n_small += 1
            for i, v in enumerate((b2, a2, g2, be2)):
                act.dma_start(par2[:, i:i + 1], v.rearrange("(p o) -> p o", o=1)).then_inc(small_in, 16)
                n_small += 1
            assert n_small == N_SMALL

            def copy_hiT(t, s):
                k = t * SLOTS + s
                act.wait_ge(hiT_full, k + 1)
                if not (isinstance(k, int) and k < 2):
                    act.wait_ge(sel_full, k - 1)
                act.activation(hiT[:, s % 2, 0:8 * POS], hiT_ps[:, s % 2, 0:8 * POS],
                               ACT.Copy).then_inc(hiT_copied, 1)

            def copy_sums(t, s):
                act.wait_ge(wsum_full, t * SLOTS + s + 1)
                k = t * 4 + s // 8
                if s % 8 == 0 and not (isinstance(k, int) and k < 2):
                    act.wait_ge(weightsum_in, NF * 16 * (k - 1))
                act.activation(wsum_ring[:, (s // 8) % 2, :, 4 * (s % 8):4 * (s % 8) + 4].rearrange("p u b -> p b u"),
                               wsum_ps[:, 0:4 * U].rearrange("p (b u) -> p b u", b=4), ACT.Copy
                               ).then_inc(wsum_copied, 1)

            def task(what, seq, t):
                misc, misc_b = bank(seq)
                act.wait_ge(misc_full, seq + 1)
                name = what if isinstance(what, str) else what[0]
                if name == "attw":
                    act.activation(vcol[:, :], misc[0:E, 0:2], ACT.Copy).then_inc(vcol_ready, 1)
                    act.activation(mapq[0:E, E:E + 1], misc[0:E, 0:1], ACT.Copy)
                    ins = act.activation(mapq[E:E + 1, :], misc[E:E + 1, 2:E + 3], ACT.Copy)
                elif name == "tableT":
                    i = what[1]
                    w = min(4, LO - 4 * i)
                    ins = act.activation(tableT[0:E, 4 * i:4 * i + w, :].rearrange("p l h -> p (l h)"),
                                         misc[0:E, 0:w * HJ], ACT.Copy)
                elif name == "w1T":
                    ins = act.activation(w1T[:, 0:2, :, :].rearrange("p g m h -> p (g m h)"), misc[0:E, 0:4 * MH], ACT.Copy)
                elif name == "w1uT":
                    ins = act.activation(w1T[0:DU, 2, :, :].rearrange("p m h -> p (m h)"), misc[0:DU, 0:2 * MH], ACT.Copy)
                elif name == "w2T":
                    ins = act.activation(w2T[:, :, :].rearrange("p m h -> p (m h)"), misc[0:MH, 0:2 * H2], ACT.Copy)
                elif name == "digit":
                    kind, hb = what[1], what[2]
                    for j in range(NF):
                        ins = act.activation(
                            digits[:, hb, kind, :, j, :].rearrange("p q (b c) -> p c q b", c=2),
                            misc_b[0:POS, 2 * j * HALF:(2 * j + 2) * HALF].rearrange("p (c q b) -> p c q b", c=2, b=2),
                            ACT.Copy)
                        if kind == 0:
                            for i, f in enumerate((ACT.Copy, ACT.Square)):
                                ins = act.activation(
                                    lo_terms[:, hb, :, j, i, :].rearrange("p q (b c) -> p c q b", c=2),
                                    misc_b[0:POS, 2 * j * HALF:(2 * j + 2) * HALF]
                                    .rearrange("p (c q b) -> p c q b", c=2, b=2), f)
                elif name == "item":
                    if not (isinstance(t, int) and t == 0):
                        act.activation(item_last[:, :], item_now[0:E, :], ACT.Copy).then_inc(item_kept, 1)
                        act.wait_ge(item_kept, t)
                    ins = act.activation(item_now[0:E, :], misc[0:E, 0:TILE], ACT.Copy)
                elif name == "query":
                    ins = act.activation(queryT[:, :], misc[0:E + 1, 0:TILE], ACT.Copy)
                elif name == "scoretab":
                    r, hb = what[1], what[2]
                    if r == 0 and not (isinstance(t, int) and t == 0 and hb == 0):
                        act.wait_ge(scoretab_in, (2 * t + hb) * (NF * 16))
                    l0, l1 = ROUNDS[r]
                    src = misc[0:HJ, 0:(l1 - l0) * HALF].rearrange("p (l q b) -> p l q b", l=l1 - l0, b=4)
                    act.activation(scores_f[:, :, l0:l1, :].rearrange("p q l b -> p l q b"), src, ACT.Copy)
                    ins = act.activation(scores_b[:, :, 0, l0:l1, :].rearrange("p q l b -> p l q b"), src, ACT.Copy)
                elif name == "finish":
                    ins = act.activation(browseT[:, :], misc[0:E, 0:TILE], ACT.Copy)
                elif name == "userT":
                    ins = act.activation(userT[:, :], misc[0:DU, 0:TILE], ACT.Copy)
                elif name == "layer1":
                    for m in range(2):
                        ins = act.activation(x1[:, m, bass.ds(t * TILE, TILE)], misc[0:MH, m * TILE:(m + 1) * TILE],
                                             ACT.Identity, bias=par1[:, 0, m:m + 1])
                ins.then_inc(misc_copied, 1)

            def lo_rows(t, n):
                k = t * STEPS + n
                hb, q0 = n // 8, (n % 8) * 4
                if n in (0, 8):
                    if isinstance(t, int) and t == 0 and n == 0:
                        act.wait_ge(misc_copied, DIGITS0)
                    elif n == 0:
                        act.wait_ge(misc_copied, misc_before(t - 1, 22) + 1)
                    else:
                        act.wait_ge(misc_copied, misc_before(t, 8) + 1)
                if not (isinstance(k, int) and k < 4):
                    act.wait_ge(wsum_full, 2 * k - 6)
                act.activation(hi_rows(n % 4)[:, :, HI:HB, :].rearrange("p g v c -> p g (v c)"),
                               lo_terms[:, hb, q0:q0 + 4, :, :, :].rearrange("p q j s c -> p (q j) (s c)"), ACT.Copy
                               ).then_inc(lo_rows_ready, 1)

            def slot(t, s, last=False):
                if s < SLOTS - 1:
                    copy_hiT(t, s + 1)
                elif not last:
                    copy_hiT(t + 1, 0)
                if s % 2 and s < SLOTS - 3:
                    lo_rows(t, s // 2 + 2)
                elif s % 2 and not last:
                    lo_rows(t + 1, s // 2 + 2 - STEPS)
                if s in in_slot:
                    what = in_slot[s]
                    if what in FIN:
                        if not (isinstance(t, int) and t == 0):
                            task(what, misc_before(t, s), t - 1)
                        else:
                            act.wait_ge(misc_copied, misc_before(t, s))
                            act.sem_inc(misc_copied, 1)
                    elif s < 16:
                        task(what, misc_before(t, s), t)
                    elif s == OWN:
                        task(what, misc_before(t, 16 if last else OWN), t)
                    elif not last:
                        task(what, misc_before(t, s), t + 1)
                if s >= SC_LAG:
                    copy_sums(t, s - SC_LAG)
                elif not (isinstance(t, int) and t == 0):
                    copy_sums(t - 1, s - SC_LAG + SLOTS)

            act.wait_ge(blk_zero, 2)
            for seq, what in enumerate(prologue):
                task(what, seq, 0)
            act.wait_ge(small_in, 16 * N_SMALL)
            lo_rows(0, 0)
            lo_rows(0, 1)
            copy_hiT(0, 0)
            for s in range(FIRST):
                slot(0, s)
            with act.Fori(0, TILES - 1) as t:
                for s in range(FIRST, SLOTS + FIRST):
                    slot(t + s // SLOTS, s % SLOTS)
            for s in range(FIRST, SLOTS):
                slot(TILES - 1, s, last=True)
            for s in range(SLOTS - SC_LAG, SLOTS):
                copy_sums(TILES - 1, s)
            base = misc_before(TILES - 1, 16) + 1
            for i, what in enumerate(FIN):
                task(what, base + i, TILES - 1)

            act.wait_ge(dve_tail, 1)
            act.activation(dice[0:MH, 0:2, 1], dice[0:MH, 0:2, 0], ACT.Sqrt).then_inc(root_ready, 1)
            act.wait_ge(dve_tail, 2)
            for q in range(4):
                for m in range(2):
                    c = slice(q * 512, (q + 1) * 512)
                    act.activation(gate1[:, m, c], x1[:, m, c], ACT.Sigmoid, bias=dice[0:MH, m, 4:5],
                                   scale=dice[0:MH, m, 3:4])
                    act.activation(norm1[:, m, c], x1[:, m, c], ACT.Identity, bias=dice[0:MH, m, 4:5],
                                   scale=dice[0:MH, m, 3:4]).then_inc(gate_ready, 1)
            for q in range(4):
                act.wait_ge(head_full, q + 1)
                act.activation(x2[:, q * 512:(q + 1) * 512], sel[0:H2, q, :], ACT.Identity,
                               bias=par2[:, 0:1]).then_inc(head_copied, 1)
            act.wait_ge(dve_tail, 3)
            act.activation(dice[0:H2, 2:3, 1], dice[0:H2, 2:3, 0], ACT.Sqrt).then_inc(root_ready, 1)
            act.wait_ge(dve_tail, 4)
            for q in range(4):
                c = slice(q * 512, (q + 1) * 512)
                act.activation(gate2[:, c], x2[:, c], ACT.Sigmoid, bias=dice[0:H2, 2, 4:5], scale=dice[0:H2, 2, 3:4])
                act.activation(norm2[:, c], x2[:, c], ACT.Identity, bias=dice[0:H2, 2, 4:5],
                               scale=dice[0:H2, 2, 3:4]).then_inc(gate_ready, 1)
            for q in range(4):
                act.wait_ge(head_full, 4 + q + 1)
                act.activation(probs[:, q * 512:(q + 1) * 512], sel[0:1, q, :], ACT.Sigmoid,
                               bias=b3s[:, :]).then_inc(head_copied, 1)

        @block.vector
        def _(dve):
            def onehot(t, n, kind):
                k = t * STEPS + n
                hb, q0 = n // 8, (n % 8) * 4
                if n in (0, 8):
                    if isinstance(t, int) and t == 0 and n == 0:
                        dve.wait_ge(misc_copied, DIGITS0)
                    elif n == 0:
                        dve.wait_ge(misc_copied, misc_before(t - 1, 23) + 1)
                    else:
                        dve.wait_ge(misc_copied, misc_before(t, 9) + 1)
                src = digits[:, hb, kind, q0:q0 + 4, :, :]
                if kind == 1:
                    if not (isinstance(k, int) and k < 4):
                        dve.wait_ge(wsum_full, 2 * k - 6)
                    dve.tensor_tensor(hi_rows(n % 4)[:, :, 0:HI, :],
                                      src.rearrange("p q j c -> p (q j) c").unsqueeze(2)
                                      .to_broadcast([POS, 4 * NF, HI, 4]),
                                      iota_hi[:, :, :].unsqueeze(1).to_broadcast([POS, 4 * NF, HI, 4]),
                                      ALU.is_equal).then_inc(hi_ready, 1)
                else:
                    if not (isinstance(k, int) and k < 2):
                        dve.wait_ge(scaled_ready, k - 1)
                    dve.tensor_tensor(onehot_lo[:, n % 2, :, :, :, :].rearrange("p q j v c -> p (q j) v c"),
                                      src.rearrange("p q j c -> p (q j) c").unsqueeze(2)
                                      .to_broadcast([POS, 4 * NF, LO, 4]),
                                      iota_lo[:, :, :].unsqueeze(1).to_broadcast([POS, 4 * NF, LO, 4]),
                                      ALU.is_equal).then_inc(lo_ready, 1)

            def pick(t, s):
                k = t * SLOTS + s
                n = s // 2
                q0 = (s % 2) * 2
                dve.wait_ge(sel_full, k + 1)
                dve.tensor_reduce(score_j[:, n % 2, q0:q0 + 2, :, :].rearrange("p q c j -> p q (c j)"),
                                  sel[0:POS, 2 * (s % 2):2 * (s % 2) + 2, 0:4 * U].rearrange("p q (c v) -> p q c v", v=LO),
                                  AX.X, ALU.max).then_inc(score_ready, 1)

            def scale(t, n):
                k = t * STEPS + n
                dve.wait_ge(lo_ready, k + 1)
                dve.wait_ge(parts_ready, k + 1)
                if not (isinstance(k, int) and k < 2):
                    dve.wait_ge(wsum_full, 2 * k - 2)
                for i in range(3):
                    ins = dve.tensor_tensor(
                        scaled_lo[:, n % 2, :, i, :, :],
                        onehot_lo[:, n % 2, :, :, :, :].rearrange("p q j v c -> p q (j v) c"),
                        parts[:, n % 2, :, i, :].unsqueeze(2).to_broadcast([POS, 4, U, 4]), ALU.mult)
                ins.then_inc(scaled_ready, 1)

            def step(t, n, last=False):
                pick(t, 2 * n + 1)
                for ahead, kind in ((2, 1), (1, 0)):
                    if n < STEPS - ahead:
                        onehot(t, n + ahead, kind)
                    elif not last:
                        onehot(t + 1, n + ahead - STEPS, kind)
                if n < STEPS - 1:
                    pick(t, 2 * n + 2)
                elif not last:
                    pick(t + 1, 0)
                scale(t, n)

            dve.memset(w2col[:, :], 0.0).then_inc(dve_tail_pre, 1)
            dve.memset(wd[:, :], 0.0).then_inc(dve_tail_pre, 1)
            dve.wait_ge(dve_tail_pre, 2)
            dve.memset(w2col[:, E:E + 1], 1.0).then_inc(attw_ready, 1)
            dve.memset(table_blk[:, :, :, :], 0.0).then_inc(blk_zero, 1)
            dve.memset(far[:, :], 0.0).then_inc(far_zero, 1)
            dve.wait_ge(far_zero, 1)
            dve.memset(far_rows[:, 2, :], -FAR).then_inc(far_made, 1)
            dve.memset(hiT[:, :, 8 * POS:], 0.0).then_inc(dve_tail_pre, 1)
            dve.memset(onehot_hi[:, :, 4 * HJ * 4:], 0.0).then_inc(dve_tail_pre, 1)
            dve.memset(tableT[E:E + 1, :, :], 0.0).then_inc(dve_tail_pre, 1)
            dve.memset(item_now[E:E + 1, :], 1.0)
            dve.wait_ge(dve_tail_pre, 5)
            dve.memset(tableT[E:E + 1, :, (NF - 1) * HB:NF * HB], 1.0).then_inc(blk_zero, 1)
            dve.wait_ge(weights_in, (NF + 3) * 16)
            flat = [wa[:, a, :, :].rearrange("p j e -> p (j e)") for a in range(4)]
            dve.tensor_tensor(wd[0:HID, 0:E], flat[1], flat[2], ALU.subtract).then_inc(attw_ready, 1)
            dve.tensor_tensor(flat[0], flat[0], flat[2], ALU.add).then_inc(attw_ready, 1)
            dve.wait_ge(vcol_ready, 1)
            dve.wait_ge(const_ready, 1)
            dve.tensor_scalar(mapq[0:E, 0:E], identf[0:E, 0:E], vcol[:, 1:2], None, ALU.mult).then_inc(mapq_ready, 1)
            for hb in range(2):
                dve.memset(scoretab[:, hb, :, :, :, :].rearrange("p q k u b -> p (q k u b)").bitcast(F32), 0.0
                           ).then_inc(scoretab_zero, 1)
            dve.wait_ge(const_ready, 2)

            onehot(0, 0, 1)
            onehot(0, 1, 1)
            onehot(0, 0, 0)
            pick(0, 0)
            for n in range(2):
                step(0, n)
            with dve.Fori(0, TILES - 1) as t:
                for n in range(2, STEPS + 2):
                    step(t + n // STEPS, n % STEPS)
            dve.wait_ge(misc_copied, misc_before(EARLY * TILES // 4 + 1, 16))
            for m in range(2):
                for q in range(EARLY):
                    dve.bn_stats(stats[0:MH, m, q, :], x1[:, m, q * 512:(q + 1) * 512])
            for n in range(2, STEPS):
                step(TILES - 1, n, last=True)

            tail_n = [5]

            def chain(ins):
                tail_n[0] += 1
                ins.then_inc(dve_tail_pre, 1)
                dve.wait_ge(dve_tail_pre, tail_n[0])

            def moments(x, rows, m0, m1, q0):
                for m in range(m0, m1):
                    for q in range(q0, 4):
                        ins = dve.bn_stats(stats[0:rows, m, q, :], x(m)[:, q * 512:(q + 1) * 512])
                chain(ins)
                for m in range(m0, m1):
                    ins = dve.bn_aggr(mv[0:rows, m, :], stats[0:rows, m, :, :].rearrange("p q s -> p (q s)"))
                chain(ins)
                dve.tensor_scalar(dice[0:rows, m0:m1, 0], mv[0:rows, m0:m1, 1], float(B) / (B - 1), EPS,
                                  ALU.mult, ALU.add).then_inc(dve_tail, 1)

            def affine(rows, m0, m1, gamma, beta, alpha):
                d = dice[0:rows, m0:m1, :]
                dve.tensor_scalar(d[:, :, 5], alpha, -1.0, 1.0, ALU.mult, ALU.add)
                chain(dve.reciprocal(d[:, :, 2], d[:, :, 1]))
                chain(dve.tensor_tensor(d[:, :, 3], d[:, :, 2], gamma, ALU.mult))
                chain(dve.tensor_tensor(d[:, :, 6], mv[0:rows, m0:m1, 0], d[:, :, 3], ALU.mult))
                dve.tensor_tensor(d[:, :, 4], beta, d[:, :, 6], ALU.subtract).then_inc(dve_tail, 1)

            dve.wait_ge(misc_copied, misc_before(TILES - 1, 16) + 1 + len(FIN))
            moments(lambda m: x1[:, m, :], MH, 0, 2, EARLY)
            dve.wait_ge(root_ready, 1)
            affine(MH, 0, 2, par1[:, 2, :], par1[:, 3, :], par1[:, 1, :])
            for q in range(4):
                for m in range(2):
                    c = slice(q * 512, (q + 1) * 512)
                    dve.wait_ge(gate_ready, 2 * q + m + 1)
                    chain(dve.tensor_scalar(gate1[:, m, c], gate1[:, m, c], dice[0:MH, m, 5:6], par1[:, 1, m:m + 1],
                                            ALU.mult, ALU.add))
                    dve.tensor_tensor(norm1[:, m, c], norm1[:, m, c], gate1[:, m, c], ALU.mult).then_inc(y_ready, 1)
            dve.wait_ge(head_copied, 4)
            moments(lambda m: x2, H2, 2, 3, 0)
            dve.wait_ge(root_ready, 2)
            affine(H2, 2, 3, par2[:, 2:3], par2[:, 3:4], par2[:, 1:2])
            for q in range(4):
                c = slice(q * 512, (q + 1) * 512)
                dve.wait_ge(gate_ready, 8 + q + 1)
                chain(dve.tensor_scalar(gate2[:, c], gate2[:, c], dice[0:H2, 2, 5:6], par2[:, 1:2], ALU.mult, ALU.add))
                dve.tensor_tensor(norm2[:, c], norm2[:, c], gate2[:, c], ALU.mult).then_inc(y_ready, 1)


_INS = ['r_user', 'r_item', 'r_rec_his', 'L0_rec_table_user', 'L0_rec_table_i1', 'L0_rec_table_i2',
        'L0_rec_table_i3', 'L0_rec_w_att1', 'L0_rec_b_att1', 'L0_rec_w_att2', 'L0_rec_b_att2', 'L0_rec_w1',
        'L0_rec_b1', 'L0_rec_a1', 'L0_rec_g1', 'L0_rec_be1', 'L0_rec_w2', 'L0_rec_b2', 'L0_rec_a2',
        'L0_rec_g2', 'L0_rec_be2', 'L0_rec_w3', 'L0_rec_b3']


def kernel(**inputs):
    import numpy as np
    import concourse.bacc as bacc
    from concourse.bass_utils import run_bass_kernel_spmd

    nc = bacc.Bacc("TRN2", target_bir_lowering=False, num_devices=1)
    arrays, args = {}, []
    for name in _INS:
        a = np.ascontiguousarray(inputs[name])
        arrays[f"in_{name}_dram"] = a
        args.append(nc.dram_tensor(f"in_{name}_dram", a.shape, mybir.dt.from_np(a.dtype), kind="ExternalInput").ap())
    rows = inputs["r_user"].shape[0]
    out = nc.dram_tensor("out_0_dram", (rows,), F32, kind="ExternalOutput").ap()
    build(nc, *args, out)
    r = run_bass_kernel_spmd(nc, [arrays], core_ids=[0])
    return r.results[0]["out_0_dram"]
```
